# Optimizing a Trainium2 kernel written in Bass

```python
import numpy as np
import jax
import jax.numpy as jnp

def _softmax(x, axis=-1):
    return jax.nn.softmax(x, axis=axis)

def _gelu(x):
    return jax.nn.gelu(x, approximate=True)

def _silu(x):
    return jax.nn.silu(x)

def _sigmoid(x):
    return jax.nn.sigmoid(x)

def _layernorm(x, axis=-1, eps=1e-05):
    m = jnp.mean(x, axis=axis, keepdims=True)
    v = jnp.var(x, axis=axis, keepdims=True)
    return (x - m) / jnp.sqrt(v + eps)

def _scatter_add(tgt, idx, src, axis=0):
    return tgt.at[idx].add(src)

def _segment_sum(src, seg, n):
    return jax.ops.segment_sum(src, seg, n)
kernel_name = 'mk_xattn_ffn_d1_seqx_r8_0ba293'

def setup_inputs(seed: int=0):
    np.random.seed(seed)
    _w = jnp.asarray

    def _rec_inputs():
        import jax
        import jax.numpy as jnp
        _rk = jax.random.key(seed)
        x = -0.000125 + 0.9999 * jax.random.normal(jax.random.fold_in(_rk, 1), (32, 64, 512), jnp.float32)
        _lenS = 64 - jax.random.randint(jax.random.fold_in(_rk, 7), (32,), 0, max(1, 64 // 4) + 1, jnp.int32)
        _lenS2 = 64 - jax.random.randint(jax.random.fold_in(_rk, 8), (32,), 0, max(1, 64 // 4) + 1, jnp.int32)
        _ctx_4096P = jax.random.normal(jax.random.fold_in(_rk, 11), (32, 16, 512), jnp.float32)
        _ctx_4096c = jax.random.dirichlet(jax.random.fold_in(_rk, 511), 0.3 * jnp.ones((16,), jnp.float32), (32, 64))
        _ctx_4096t = jnp.einsum('bsk,bkd->bsd', _ctx_4096c, _ctx_4096P)
        _ctx_4096t = _ctx_4096t * jax.lax.rsqrt(jnp.mean(jnp.square(_ctx_4096t)) + 1e-12) * 0.953939
        ctx_4096 = -1.52775e-05 + 0.999936 * (_ctx_4096t + 0.3 * jax.random.normal(jax.random.fold_in(_rk, 611), (32, 64, 512), jnp.float32))
        return (x, ctx_4096)
    x, ctx_4096 = _rec_inputs()

    def _L0_xattn_setup():
        import jax, jax.numpy as jnp
        import numpy as np
        NUM_HEADS = 8

        def _proj(W, b, x):
            return jnp.einsum('oi,bil->bol', W, x) + b[:, None]
        key = jax.random.key(seed)
        ks = jax.random.split(key, 11)
        B, D, L = (16, 64, 512)
        s = 1.0 / np.sqrt(D).astype(np.float32)
        return {'x_query': jax.random.normal(ks[0], (B, D, L), jnp.float32), 'x_key': jax.random.normal(ks[1], (B, D, L), jnp.float32), 'x_value': jax.random.normal(ks[2], (B, D, L), jnp.float32), 'Wq': jax.random.normal(ks[3], (D, D), jnp.float32) * s, 'bq': jax.random.normal(ks[4], (D,), jnp.float32) * 0.01, 'Wk': jax.random.normal(ks[5], (D, D), jnp.float32) * s, 'bk': jax.random.normal(ks[6], (D,), jnp.float32) * 0.01, 'Wv': jax.random.normal(ks[7], (D, D), jnp.float32) * s, 'bv': jax.random.normal(ks[8], (D,), jnp.float32) * 0.01, 'Wo': jax.random.normal(ks[9], (D, D), jnp.float32) * s, 'bo': jax.random.normal(ks[10], (D,), jnp.float32) * 0.01}
    _L0_xattn_all = _L0_xattn_setup()
    _L0_xattn_in = {k: v for k, v in _L0_xattn_all.items() if k in ('Wq', 'bq', 'Wk', 'bk', 'Wv', 'bv', 'Wo', 'bo')}
    del _L0_xattn_all

    def _L0_ffn_setup():
        import jax, jax.numpy as jnp
        import numpy as np
        GROUP_SIZE = 128

        def dequantize(imatrix, scales, zeros, group_size, out_dtype):
            rs = jnp.repeat(scales, group_size, axis=0)
            rz = jnp.repeat(zeros, group_size, axis=0)
            return ((imatrix.astype(rs.dtype) - rz.astype(rs.dtype)) * rs).astype(out_dtype)
        key = jax.random.key(seed)
        ks = jax.random.split(key, 10)
        H, I, G = (512, 1792, GROUP_SIZE)
        B, S = (4, 256)
        x = jax.random.normal(ks[0], (B, S, H), dtype=jnp.float32)
        gate_w = jax.random.randint(ks[1], (H, I), 0, 16, dtype=jnp.int32)
        gate_z = jax.random.randint(ks[2], (H // G, I), 0, 16, dtype=jnp.int32)
        gate_s = jax.random.uniform(ks[3], (H // G, I), dtype=jnp.float32) * 0.01
        up_w = jax.random.randint(ks[4], (H, I), 0, 16, dtype=jnp.int32)
        up_z = jax.random.randint(ks[5], (H // G, I), 0, 16, dtype=jnp.int32)
        up_s = jax.random.uniform(ks[6], (H // G, I), dtype=jnp.float32) * 0.01
        down_w = jax.random.randint(ks[7], (I, H), 0, 16, dtype=jnp.int32)
        down_z = jax.random.randint(ks[8], (I // G, H), 0, 16, dtype=jnp.int32)
        down_s = jax.random.uniform(ks[9], (I // G, H), dtype=jnp.float32) * 0.01
        return {'x': x, 'gate_w': gate_w, 'gate_z': gate_z, 'gate_s': gate_s, 'up_w': up_w, 'up_z': up_z, 'up_s': up_s, 'down_w': down_w, 'down_z': down_z, 'down_s': down_s}
    _L0_ffn_all = _L0_ffn_setup()
    _L0_ffn_in = {k: v for k, v in _L0_ffn_all.items() if k in ('gate_w', 'gate_z', 'gate_s', 'up_w', 'up_z', 'up_s', 'down_w', 'down_z', 'down_s')}
    del _L0_ffn_all
    return {'x': x, 'ctx_4096': ctx_4096, 'L0_xattn_Wq': _L0_xattn_in['Wq'], 'L0_xattn_bq': _L0_xattn_in['bq'], 'L0_xattn_Wk': _L0_xattn_in['Wk'], 'L0_xattn_bk': _L0_xattn_in['bk'], 'L0_xattn_Wv': _L0_xattn_in['Wv'], 'L0_xattn_bv': _L0_xattn_in['bv'], 'L0_xattn_Wo': _L0_xattn_in['Wo'], 'L0_xattn_bo': _L0_xattn_in['bo'], 'L0_ffn_gate_w': _L0_ffn_in['gate_w'], 'L0_ffn_gate_z': _L0_ffn_in['gate_z'], 'L0_ffn_gate_s': _L0_ffn_in['gate_s'], 'L0_ffn_up_w': _L0_ffn_in['up_w'], 'L0_ffn_up_z': _L0_ffn_in['up_z'], 'L0_ffn_up_s': _L0_ffn_in['up_s'], 'L0_ffn_down_w': _L0_ffn_in['down_w'], 'L0_ffn_down_z': _L0_ffn_in['down_z'], 'L0_ffn_down_s': _L0_ffn_in['down_s']}

def reference(x, ctx_4096, L0_xattn_Wq, L0_xattn_bq, L0_xattn_Wk, L0_xattn_bk, L0_xattn_Wv, L0_xattn_bv, L0_xattn_Wo, L0_xattn_bo, L0_ffn_gate_w, L0_ffn_gate_z, L0_ffn_gate_s, L0_ffn_up_w, L0_ffn_up_z, L0_ffn_up_s, L0_ffn_down_w, L0_ffn_down_z, L0_ffn_down_s):
    import jax
    import jax.numpy as jnp

    def _L0_xattn_ref(x_query, x_key, x_value, Wq, bq, Wk, bk, Wv, bv, Wo, bo):
        import jax, jax.numpy as jnp
        import numpy as np
        NUM_HEADS = 8

        def _proj(W, b, x):
            return jnp.einsum('oi,bil->bol', W, x) + b[:, None]
        B, D, L = x_query.shape
        h = NUM_HEADS
        Lh = L // h
        q = _proj(Wq, bq, x_query)
        k = _proj(Wk, bk, x_key)
        v = _proj(Wv, bv, x_value)
        qh = q.reshape(B, D, h, Lh).transpose(2, 0, 1, 3)
        kh = k.reshape(B, D, h, Lh).transpose(2, 0, 1, 3)
        vh = v.reshape(B, D, h, Lh).transpose(2, 0, 1, 3)
        scale = 1.0 / jnp.sqrt(jnp.asarray(Lh, x_query.dtype))
        scores = jnp.einsum('hbdk,hbek->hbde', qh, kh) * scale
        p = jax.nn.softmax(scores, axis=-1)
        xh = jnp.einsum('hbde,hbek->hbdk', p, vh)
        x = xh.transpose(1, 2, 0, 3).reshape(B, D, L)
        return _proj(Wo, bo, x)

    def _L0_ffn_ref(x, gate_w, gate_z, gate_s, up_w, up_z, up_s, down_w, down_z, down_s):
        import jax, jax.numpy as jnp
        import numpy as np
        GROUP_SIZE = 128

        def dequantize(imatrix, scales, zeros, group_size, out_dtype):
            rs = jnp.repeat(scales, group_size, axis=0)
            rz = jnp.repeat(zeros, group_size, axis=0)
            return ((imatrix.astype(rs.dtype) - rz.astype(rs.dtype)) * rs).astype(out_dtype)
        dt = x.dtype
        gate_proj = dequantize(gate_w, gate_s, gate_z, GROUP_SIZE, dt)
        up_proj = dequantize(up_w, up_s, up_z, GROUP_SIZE, dt)
        down_proj = dequantize(down_w, down_s, down_z, GROUP_SIZE, dt)
        gate = jax.nn.silu(jnp.dot(x, gate_proj))
        up = jnp.dot(x, up_proj)
        return jnp.dot(gate * up, down_proj)
    x = x + _L0_xattn_ref(_layernorm(x, axis=-1), ctx_4096, ctx_4096, L0_xattn_Wq, L0_xattn_bq, L0_xattn_Wk, L0_xattn_bk, L0_xattn_Wv, L0_xattn_bv, L0_xattn_Wo, L0_xattn_bo)
    x = x + _L0_ffn_ref(_layernorm(x, axis=-1), L0_ffn_gate_w, L0_ffn_gate_z, L0_ffn_gate_s, L0_ffn_up_w, L0_ffn_up_z, L0_ffn_up_s, L0_ffn_down_w, L0_ffn_down_z, L0_ffn_down_s)
    return x

_drawn_inputs = setup_inputs


def setup_inputs(seed=0):
    import zlib

    import numpy as np

    out = dict(_drawn_inputs(seed))
    spreads = {}
    factors = {'L0_xattn_bq': 22.105, 'L0_xattn_bk': 8.0, 'L0_xattn_bv': 8.0, 'L0_xattn_bo': 6.107}
    for name, (base, spread) in spreads.items():
        noise = np.random.default_rng([zlib.crc32(name.encode()), seed]).standard_normal(out[name].shape)
        drawn = base * np.exp(spread * noise) if base else spread * noise
        out[name] = jnp.asarray(drawn.astype(out[name].dtype))
    for name, factor in factors.items():
        out[name] = (out[name] * factor).astype(out[name].dtype)
    return out
```

```python
from contextlib import ExitStack

import concourse.bass as bass
from concourse import mybir

F32 = mybir.dt.float32
F32R = mybir.dt.float32r
I32 = mybir.dt.int32
ALU = mybir.AluOpType
ACT = mybir.ActivationFunctionType
AX_X = mybir.AxisListType.X

P = 128
EPS = 1e-5


def xattn_ffn(nc, x, ctx, Wq, bq, Wk, bk, Wv, bv, Wo, bo,
              gate_w, gate_z, gate_s, up_w, up_z, up_s, down_w, down_z, down_s, out):
    B, D, L = x.shape
    Lh = 64
    NC = L // P
    NT = B * D // P
    I = gate_w.shape[1]
    NG = L // P
    NI = I // P
    CT = 4
    NCH = NT // CT
    CR = CT * P
    NS = NCH * NI
    SCALE = 1.0 / Lh ** 0.5
    assert 2 * D == P and L == 512 and CR == 512 and down_w.shape == (I, L)

    HALF = I // 2
    pieces = []
    for m, (w, z) in enumerate(((gate_w, gate_z), (up_w, up_z))):
        for g in range(NG):
            for a in range(2):
                cols = slice(a * HALF, (a + 1) * HALF)
                pieces.append((w[g * P:(g + 1) * P, cols], z[g:g + 1, cols], HALF, ("gu", m, g, cols)))
    for g in range(NI):
        pieces.append((down_w[g * P:(g + 1) * P, :], down_z[g:g + 1, :], L, ("d", 0, g, slice(0, L))))
    RING = 3
    NSMALL = 2 + 4 + 3 + 10

    with ExitStack() as keep:
        def sem(name):
            return keep.enter_context(nc.semaphore(name))

        def sb(name, shape, dt=F32, stack=keep):
            return stack.enter_context(nc.sbuf_tensor(name, shape, dt))

        x_sb = sb("x_sb", [P, NT, L])
        wgu = sb("wgu", [P, 2, NG, I], F32R)
        wd = sb("wd", [P, NI, L], F32R)
        xT = sb("xT", [P, 2, 2, NG, CR], F32R)
        xn2 = sb("xn2", [P, 2, L])
        ident = sb("ident", [P, P])
        wraw = sb("wraw", [P, 4, P])
        wT = sb("wT", [P, 4, P])
        bqk = sb("bqk", [P, 2, D])
        bvo = sb("bvo", [P, 2])
        s_raw = sb("s_raw", [P, 2, P])
        sgu = sb("sgu", [P, 2, NG, NI])
        sd = sb("sd", [P, NI, NC])
        st6 = sb("st6", [P, 2, 6])
        mv = sb("mv", [P, 2, NT, 2])
        ve = sb("ve", [P, 2, NT])
        rs = sb("rs", [P, 2, NT])
        power = sb("power", [P, 1])
        mx = sb("mx", [P, 2 * NC])
        sm = sb("sm", [P, 2 * NC])
        ri = sb("ri", [P, 2 * NC])

        CTXB = 2
        with ExitStack() as s1:
            ctx_sb = sb("ctx_sb", [P, CTXB, L], F32, s1)
            xn = sb("xn", [P, 2, L], F32, s1)
            qT = sb("qT", [P, NC, P], F32, s1)
            kT = sb("kT", [P, NC, P], F32, s1)
            v_sb = sb("v_sb", [P, 2, 2, L], F32, s1)
            pe_ = sb("pe_", [P, NC, 2, Lh], F32, s1)
            p_sb = sb("p_sb", [P, NC, 2, Lh], F32, s1)
            aT = sb("aT", [P, NC, P], F32, s1)
            w_in = sb("w_in", [P, RING, 2, HALF], I32, s1)
        with ExitStack() as s2:
            acc = sb("acc", [P, 2, 2, 2, CR], F32, s2)
            hr = sb("hr", [P, 2, 2, CR], F32R, s2)
            yT = sb("yT", [P, 2, NC, CR], F32, s2)

        banks = keep.enter_context(nc.psum_tensor("banks", [P, 8, 512], F32))
        BQ, BK, BV, BS, BA, BO = 0, 1, 2, 3, 5, 6

        s_zero = sem("s_zero")
        s_small = sem("s_small")
        s_id = sem("s_id")
        s_x = [sem(f"s_xin{i}") for i in range(6)]
        s_ctx = [sem(f"s_ctx{i}") for i in range(CTXB)]
        s_w = [sem(f"s_w{i}") for i in range(RING)]
        s_cv = sem("s_cv")
        s_deq = sem("s_deq")
        s_tr = sem("s_tr")
        s_wT = sem("s_wT")
        s_ln = sem("s_ln")
        s_var = [sem("s_var1"), sem("s_var2")]
        s_rs = [sem("s_rs1"), sem("s_rs2")]
        s_xn = sem("s_xn")
        s_q = sem("s_q")
        s_k = sem("s_k")
        s_v = sem("s_v")
        s_qe = sem("s_qe")
        s_ke = sem("s_ke")
        s_ve = sem("s_ve")
        s_s = sem("s_s")
        s_mx = sem("s_mx")
        s_sub = sem("s_sub")
        s_exp = sem("s_exp")
        s_sum = sem("s_sum")
        s_ri = sem("s_ri")
        s_p = sem("s_p")
        s_at = sem("s_at")
        s_ate = sem("s_ate")
        s_o = sem("s_o")
        s_x1 = sem("s_x1")
        s_xn2 = sem("s_xn2")
        s_fill = sem("s_fill")
        s_ea = sem("s_ea")
        s_ev = sem("s_ev")
        s_xhi = sem("s_xhi")
        s_silu = sem("s_silu")
        s_hi = sem("s_hi")
        s_add = sem("s_add")
        s_h = sem("s_h")
        s_lo = sem("s_lo")
        s_out = sem("s_out")

        xf = x.rearrange("b d l -> (b d) l").rearrange("(t p) l -> p t l", p=P)
        cf = ctx.rearrange("b d l -> (b d) l").rearrange("(t p) l -> p t l", p=P)
        of = out.rearrange("b d l -> (b d) l").rearrange("(t p) l -> p t l", p=P)

        xparts = [(0, 1), (1, 2), (2, 4), (4, 8), (8, 12), (12, 16)]
        xpart = {t: i for i, (a, b) in enumerate(xparts) for t in range(a, b)}

        uses = [("X", 0, t) for t in range(CT)]
        for n in range(NS + 2):
            c, it = divmod(n, NI)
            for g in range(NG):
                if n < NS:
                    uses += [("G", n, g), ("U", n, g)]
                if n >= 2:
                    uses.append(("D", n - 2, g))
            if c + 1 < NCH and 6 <= it < 6 + CT:
                uses.append(("X", c + 1, it - 6))
            if 0 < c < NCH and 3 <= it < 3 + CT:
                uses.append(("Y", c - 1, it - 3))
        uses += [("Y", NCH - 1, t) for t in range(CT)]
        index = {u: i for i, u in enumerate(uses)}

        def reader(u):
            kind, n, g = u
            if kind in "GU" and g < 2 or kind == "D" and n % NI == 0:
                return "scalar"
            return "vector"

        freed, count = {}, {"scalar": 0, "vector": 0}
        for u in uses:
            count[reader(u)] += 1
            freed[u] = count[reader(u)]
        read_sem = {"scalar": s_ea, "vector": s_ev}

        def wait_read(eng, u):
            eng.wait_ge(read_sem[reader(u)], freed[u])

        def scale_of(u):
            kind, n, g = u
            it = n % NI
            return sd[:, it, g:g + 1] if kind == "D" else sgu[:, "GU".index(kind), g, it:it + 1]

        block = keep.enter_context(nc.Block())

        @block.sync
        def _(sp):
            def load_x(i):
                a, b = xparts[i]
                sp.dma_start(x_sb[:, a:b, :], xf[:, a:b, :]).then_inc(s_x[i], 16)

            def load_ctx(j):
                if j >= CTXB:
                    sp.wait_ge(s_k, j - CTXB + 1)
                    sp.wait_ge(s_v, 2 * (j - CTXB + 1))
                sp.dma_start(ctx_sb[:, j % CTXB, :], cf[:, j, :]).then_inc(s_ctx[j % CTXB], 16)

            def load_piece(k):
                w, z, n, _ = pieces[k]
                if k >= RING:
                    sp.wait_ge(s_deq, k - RING + 1)
                sp.dma_start(w_in[:, k % RING, 0, 0:n], w).then_inc(s_w[k % RING], 16)
                sp.dma_start(w_in[:, k % RING, 1, 0:n], z.partition_broadcast(P)).then_inc(s_w[k % RING], 16)

            load_x(0)
            load_ctx(0)
            load_x(1)
            load_ctx(1)
            load_x(2)
            load_x(3)
            k = 0
            for j in range(NT):
                if j in (1, 4):
                    load_x(4 + j // 4)
                while k < min(len(pieces), 2 * j + 3):
                    load_piece(k)
                    k += 1
                if j + CTXB < NT:
                    load_ctx(j + CTXB)
            while k < len(pieces):
                load_piece(k)
                k += 1
            for t in range(NT):
                wait_read(sp, ("Y", t // CT, t % CT))
                sp.dma_start(of[:, t, :], x_sb[:, t, :]).then_inc(s_out, 16)
            sp.wait_ge(s_out, 16 * NT)

        @block.gpsimd
        def _(pool):
            pool.memset(ident[:, :], 0.0).then_inc(s_id, 1)
            pool.wait_ge(s_id, 1)
            pool.affine_select(out=ident[:, :], in_=ident[:, :], compare_op=ALU.not_equal, fill=1.0,
                               base=0, pattern=[[-1, P]], channel_multiplier=1).then_inc(s_id, 1)
            pool.memset(power[:, :], -0.5).then_inc(s_id, 1)
            pool.wait_ge(s_id, 3)

            def rstd(m, j):
                pool.wait_ge(s_var[m], j + 1)
                pool.tensor_tensor(rs[:, m, j:j + 1], ve[:, m, j:j + 1], power[:, :], ALU.pow).then_inc(s_rs[m], 1)

            def dequantise(k):
                _, _, n, (where, m, g, cols) = pieces[k]
                pool.wait_ge(s_cv, k + 1)
                dst = wgu[:, m, g, cols] if where == "gu" else wd[:, g, cols]
                pool.tensor_tensor(dst, w_in[:, k % RING, 0, 0:n].bitcast(F32), w_in[:, k % RING, 1, 0:n].bitcast(F32),
                                   ALU.subtract).then_inc(s_deq, 1)

            rstd(0, 0)
            rstd(0, 1)
            for j in range(NT):
                if j + 2 < NT:
                    rstd(0, j + 2)
                if j >= 1:
                    rstd(1, j - 1)
                for k in range(2 * j, min(2 * j + 2, len(pieces))):
                    dequantise(k)
            rstd(1, NT - 1)

            for n in range(NS + 1):
                if n > 0:
                    m = (n - 1) % 2
                    pool.wait_ge(s_silu, n)
                    wait_read(pool, ("U", n - 1, NG - 1))
                    pool.tensor_tensor(acc[:, m, 1, 0, :], acc[:, m, 0, 0, :], acc[:, m, 1, 0, :],
                                       ALU.mult).then_inc(s_h, 1)
                if n < NS:
                    for a, kind in enumerate("GU"):
                        wait_read(pool, (kind, n, 1))
                        pool.tensor_tensor(acc[:, n % 2, a, 0, :], acc[:, n % 2, a, 0, :],
                                           acc[:, n % 2, a, 1, :], ALU.add).then_inc(s_add, 1)
                if n > 0:
                    pool.wait_ge(s_hi, n)
                    pool.tensor_tensor(hr[:, m, 1, :], acc[:, m, 1, 0, :], hr[:, m, 0, :].bitcast(F32),
                                       ALU.subtract).then_inc(s_lo, 1)

        @block.scalar
        def _(act):
            small = [(bqk[:, 0, :], bq.rearrange("(a o) -> a o", a=1).partition_broadcast(P)),
                     (bqk[:, 1, :], bk.rearrange("(a o) -> a o", a=1).partition_broadcast(P))]
            col = lambda v: v.rearrange("(o a) -> o a", a=1)
            for h in range(2):
                rows = slice(h * D, (h + 1) * D)
                small += [(bvo[rows, 0:1], col(bv)), (bvo[rows, 1:2], col(bo))]
            rows_of = lambda s: s.rearrange("g (t p) -> (g t) p", p=P)
            small += [(s_raw[0:NG * NI, 0, :], rows_of(gate_s)),
                      (s_raw[NG * NI:2 * NG * NI, 0, :], rows_of(up_s)),
                      (s_raw[0:NI * NC, 1, :], rows_of(down_s))]
            late = []
            for m, w in enumerate((Wq, Wk, Wo, Wv)):
                for a in range(2):
                    for b in range(2):
                        if a == b or w is Wv:
                            late.append((wraw[a * D:(a + 1) * D, m, b * D:(b + 1) * D], w))
            for dst, src in small:
                act.dma_start(dst, src).then_inc(s_small, 16)
            act.wait_ge(s_zero, 1)
            for dst, src in late:
                act.dma_start(dst, src).then_inc(s_small, 16)
            assert len(small) + len(late) == NSMALL

            def take_v(j, b):
                act.wait_ge(s_v, 2 * j + b + 1)
                if j >= 2:
                    act.wait_ge(s_o, j - 1)
                act.activation(v_sb[:, j % 2, b, :], banks[:, BV, :], ACT.Identity,
                               bias=bvo[:, 0:1]).then_inc(s_ve, 1)

            def convert(k):
                n = pieces[k][2]
                act.wait_ge(s_w[k % RING], 32 * (k // RING + 1))
                act.copy(w_in[:, k % RING, :, 0:n].bitcast(F32), w_in[:, k % RING, :, 0:n]).then_inc(s_cv, 1)

            act.wait_ge(s_small, 16 * NSMALL)
            take_v(0, 0)
            take_v(0, 1)
            for j in range(NT):
                act.wait_ge(s_sub, j + 1)
                act.activation(pe_[:, :, :, :], pe_[:, :, :, :], ACT.Exp, scale=SCALE).then_inc(s_exp, 1)
                if j + 1 < NT:
                    take_v(j + 1, 0)
                    take_v(j + 1, 1)
                for k in range(2 * j, min(2 * j + 2, len(pieces))):
                    convert(k)
                act.wait_ge(s_at, j + 1)
                act.copy(aT[:, :, :], banks[:, BA, :].rearrange("p (c o) -> p c o", c=NC)).then_inc(s_ate, 1)

            act.wait_ge(s_x1, NT)
            act.wait_ge(s_deq, len(pieces))

            def silu(n):
                wait_read(act, ("G", n, NG - 1))
                act.activation(acc[:, n % 2, 0, 0, :], acc[:, n % 2, 0, 0, :], ACT.Silu).then_inc(s_silu, 1)

            def high(n):
                act.wait_ge(s_h, n + 1)
                if n >= 2:
                    act.wait_ge(s_fill, index[("D", n - 2, NC - 1)] + 1)
                act.copy(hr[:, n % 2, 0, :], acc[:, n % 2, 1, 0, :]).then_inc(s_hi, 1)

            for u in uses:
                kind, n, g = u
                if kind == "X":
                    act.wait_ge(s_fill, index[u] + 1)
                    act.copy(xT[:, n % 2, 0, :, g * P:(g + 1) * P],
                             banks[:, index[u] % 8, :].rearrange("p (g r) -> p g r", g=NG)).then_inc(s_xhi, 1)
                if reader(u) == "scalar":
                    act.wait_ge(s_fill, index[u] + 1)
                    if kind == "G" and g == 0 and n >= 2:
                        act.wait_ge(s_lo, n - 1)
                    dst = yT[:, n // NI % 2, g, :] if kind == "D" else acc[:, n % 2, "GU".index(kind), g, :]
                    act.activation(dst, banks[:, index[u] % 8, :], ACT.Copy,
                                   scale=scale_of(u)).then_inc(s_ea, 1)
                if kind == "G" and g == 0 and n > 0:
                    silu(n - 1)
                if kind == "U" and g == 1 and n > 0:
                    high(n - 1)
                if u == ("U", NS - 1, NG - 1):
                    silu(NS - 1)
                    high(NS - 1)

        @block.tensor
        def _(pe):
            pe.wait_ge(s_id, 2)
            pe.wait_ge(s_small, 16 * NSMALL)
            for m in range(4):
                pe.transpose(banks[:, 0, m * P:(m + 1) * P], wraw[:, m, :], ident[:, :])
            ng, nd = 2 * NG * NI, NI * NC
            pe.transpose(banks[:, 1, 0:ng], s_raw[0:ng, 0, :], ident[0:ng, 0:ng])
            pe.transpose(banks[:, 1, ng:ng + nd], s_raw[0:nd, 1, :], ident[0:nd, 0:nd]).then_inc(s_tr, 1)
            pe.wait_ge(s_wT, 2)

            def project(j):
                c = j % CTXB
                pe.wait_ge(s_xn, j + 1)
                if j >= 1:
                    pe.wait_ge(s_qe, j)
                for b in range(NC):
                    mm = pe.matmul(banks[:, BQ, b * P:(b + 1) * P], xn[:, j % 2, b * P:(b + 1) * P],
                                   wT[:, 0, :], start=True, stop=True)
                mm.then_inc(s_q, 1)
                pe.wait_ge(s_ctx[c], 16 * (j // CTXB + 1))
                for h in range(2):
                    if 2 * j + h > 0:
                        pe.wait_ge(s_ve, 2 * j + h)
                    r = slice(h * D, (h + 1) * D)
                    pe.matmul(banks[:, BV, :], wT[r, 3, :], ctx_sb[r, c, :],
                              start=True, stop=True).then_inc(s_v, 1)
                    if h == 0:
                        if j >= 1:
                            pe.wait_ge(s_ke, j)
                        for b in range(NC):
                            mm = pe.matmul(banks[:, BK, b * P:(b + 1) * P], ctx_sb[:, c, b * P:(b + 1) * P],
                                           wT[:, 1, :], start=True, stop=True)
                        mm.then_inc(s_k, 1)

            def scores(j):
                pe.wait_ge(s_qe, j + 1)
                pe.wait_ge(s_ke, j + 1)
                if j >= 1:
                    pe.wait_ge(s_sub, j)
                for c in range(NC):
                    for h in range(2):
                        r = slice(h * Lh, (h + 1) * Lh)
                        for b in range(2):
                            o = slice(b * D, (b + 1) * D)
                            mm = pe.matmul(banks[o, BS + h, c * D:(c + 1) * D], qT[r, c, o], kT[r, c, o],
                                           start=True, stop=True)
                mm.then_inc(s_s, 1)

            def mix(j):
                pe.wait_ge(s_p, j + 1)
                if j >= 1:
                    pe.wait_ge(s_ate, j)
                for c in range(NC):
                    mm = pe.matmul(banks[:, BA, c * P:(c + 1) * P],
                                   p_sb[:, c, :, :].rearrange("p h e -> p (h e)"), wT[:, 2, :],
                                   start=True, stop=True)
                mm.then_inc(s_at, 1)

            def apply(j):
                pe.wait_ge(s_ate, j + 1)
                pe.wait_ge(s_ve, 2 * j + 2)
                if j >= 1:
                    pe.wait_ge(s_x1, j)
                for c in range(NC):
                    for h in range(2):
                        r = slice(h * Lh, (h + 1) * Lh)
                        for b in range(2):
                            o = slice(b * D, (b + 1) * D)
                            lo = (2 * c + h) * Lh
                            mm = pe.matmul(banks[o, BO + h, c * Lh:(c + 1) * Lh], aT[r, c, o],
                                           v_sb[r, j % 2, b, lo:lo + Lh], start=True, stop=True)
                mm.then_inc(s_o, 1)

            project(0)
            for j in range(NT):
                scores(j)
                if j >= 1:
                    apply(j - 1)
                if j + 1 < NT:
                    project(j + 1)
                mix(j)
            apply(NT - 1)

            pe.wait_ge(s_deq, len(pieces))
            pe.wait_ge(s_x1, NT)
            for i, u in enumerate(uses):
                kind, n, g = u
                bank = banks[:, i % 8, :]
                if i >= 8:
                    wait_read(pe, uses[i - 8])
                if kind == "X":
                    pe.wait_ge(s_xn2, n * CT + g + 1)
                    for b in range(NG):
                        mm = pe.transpose(bank[:, b * P:(b + 1) * P], xn2[:, g % 2, b * P:(b + 1) * P], ident[:, :])
                elif kind == "Y":
                    if g == 0:
                        wait_read(pe, ("D", n * NI + NI - 1, NC - 1))
                    for b in range(NC):
                        mm = pe.transpose(bank[:, b * P:(b + 1) * P], yT[:, n % 2, b, g * P:(g + 1) * P], ident[:, :])
                else:
                    c, it = divmod(n, NI)
                    if kind == "D":
                        if g == 0:
                            pe.wait_ge(s_lo, n + 1)
                        w = wd[:, it, g * P:(g + 1) * P]
                        parts = [hr[:, n % 2, part, :] for part in range(2)]
                    else:
                        if kind == "G" and g == 0 and it == 0:
                            wait_read(pe, ("X", c, CT - 1))
                        w = wgu[:, "GU".index(kind), g, it * P:(it + 1) * P]
                        parts = [xT[:, c % 2, part, g, :] for part in range(2)]
                    pe.matmul(bank, w, parts[0], start=True, stop=False)
                    mm = pe.matmul(bank, w, parts[1], start=False, stop=True)
                mm.then_inc(s_fill, 1)

        @block.vector
        def _(dve):
            steps = [0]

            def chain(ins):
                steps[0] += 1
                ins.then_inc(s_ln, 1)
                dve.wait_ge(s_ln, steps[0])

            def statistics(m, j):
                chain(dve.bn_stats(st6[:, m, :], x_sb[:, j, :]))
                chain(dve.bn_aggr(mv[:, m, j, :], st6[:, m, :]))
                dve.tensor_scalar(ve[:, m, j:j + 1], mv[:, m, j, 1:2], EPS, None, ALU.add).then_inc(s_var[m], 1)

            dve.memset(wraw[:, :, :], 0.0).then_inc(s_zero, 1)

            def stats1(j):
                dve.wait_ge(s_x[xpart[j]], 16)
                statistics(0, j)

            def norm1(j):
                dve.wait_ge(s_rs[0], j + 1)
                if j >= 2:
                    dve.wait_ge(s_q, j - 1)
                dve.tensor_scalar(xn[:, j % 2, :], x_sb[:, j, :], mv[:, 0, j, 0:1], rs[:, 0, j:j + 1],
                                  ALU.subtract, ALU.mult).then_inc(s_xn, 1)

            def take(bank, dst, m, src_sem, done, j):
                dve.wait_ge(src_sem, j + 1)
                dve.tensor_tensor(dst[:, :, :].rearrange("p c (b o) -> p (c b) o", b=2),
                                  banks[:, bank, :].rearrange("p (c o) -> p c o", o=D),
                                  bqk[:, m:m + 1, :].to_broadcast([P, 2 * NC, D]), ALU.add).then_inc(done, 1)

            def heads(t):
                return t[:, :].rearrange("p (h c) -> p h c", h=2)

            S = banks[:, BS:BS + 2, 0:NC * D].rearrange("p h (c e) -> p h c e", e=D)
            E = pe_[:, :, :, :].rearrange("p c h e -> p h c e")
            PR = p_sb[:, :, :, :].rearrange("p c h e -> p h c e")

            def soft1(j):
                dve.wait_ge(s_s, j + 1)
                dve.tensor_reduce(heads(mx), S, AX_X, ALU.max).then_inc(s_mx, 1)
                dve.wait_ge(s_mx, j + 1)
                dve.tensor_tensor(E, S, heads(mx).unsqueeze(3).to_broadcast([P, 2, NC, D]),
                                  ALU.subtract).then_inc(s_sub, 1)

            def soft2(j):
                dve.wait_ge(s_exp, j + 1)
                dve.tensor_reduce(heads(sm), E, AX_X, ALU.add).then_inc(s_sum, 1)
                dve.wait_ge(s_sum, j + 1)
                dve.reciprocal(ri[:, :], sm[:, :]).then_inc(s_ri, 1)
                dve.wait_ge(s_ri, j + 1)
                if j >= 1:
                    dve.wait_ge(s_at, j)
                dve.tensor_tensor(PR, E, heads(ri).unsqueeze(3).to_broadcast([P, 2, NC, D]),
                                  ALU.mult).then_inc(s_p, 1)

            stats1(0)
            stats1(1)
            dve.wait_ge(s_tr, 1)
            dve.tensor_copy(wT[:, :, :], banks[:, 0, :].rearrange("p (m o) -> p m o", m=4)).then_inc(s_wT, 1)
            ng, nd = 2 * NG * NI, NI * NC
            dve.tensor_copy(sgu[:, :, :, :].rearrange("p a g t -> p (a g t)"), banks[:, 1, 0:ng])
            dve.tensor_copy(sd[:, :, :].rearrange("p g c -> p (g c)"), banks[:, 1, ng:ng + nd]).then_inc(s_wT, 1)
            norm1(0)
            norm1(1)
            take(BQ, qT, 0, s_q, s_qe, 0)
            take(BK, kT, 1, s_k, s_ke, 0)

            def residual(j):
                dve.wait_ge(s_o, j + 1)
                xv = x_sb[:, j, :].rearrange("p (c h l) -> p h c l", c=NC, h=2)
                for h in range(2):
                    ins = dve.scalar_tensor_tensor(
                        xv[:, h], banks[:, BO + h, 0:NC * Lh].rearrange("p (c l) -> p c l", c=NC),
                        bvo[:, 1:2], xv[:, h], ALU.add, ALU.add)
                ins.then_inc(s_x1, 1)

            def stats2(j):
                dve.wait_ge(s_x1, j + 1)
                statistics(1, j)

            for j in range(NT):
                if j + 2 < NT:
                    stats1(j + 2)
                soft1(j)
                if j >= 1:
                    residual(j - 1)
                if j + 1 < NT:
                    take(BQ, qT, 0, s_q, s_qe, j + 1)
                soft2(j)
                if j + 1 < NT:
                    take(BK, kT, 1, s_k, s_ke, j + 1)
                if j >= 1:
                    stats2(j - 1)
                if j + 2 < NT:
                    norm1(j + 2)
            residual(NT - 1)
            stats2(NT - 1)

            def norm2(t):
                dve.wait_ge(s_rs[1], t + 1)
                if t >= 2:
                    dve.wait_ge(s_fill, index[("X", (t - 2) // CT, (t - 2) % CT)] + 1)
                dve.tensor_scalar(xn2[:, t % 2, :], x_sb[:, t, :], mv[:, 1, t, 0:1], rs[:, 1, t:t + 1],
                                  ALU.subtract, ALU.mult).then_inc(s_xn2, 1)

            norm2(0)
            norm2(1)
            for u in uses:
                kind, n, g = u
                if kind == "G" and g == 0:
                    c, it = divmod(n, NI)
                    if c + 1 < NCH and it in (4, 5):
                        norm2((c + 1) * CT + it - 4)
                if reader(u) == "scalar":
                    continue
                bank = banks[:, index[u] % 8, :]
                dve.wait_ge(s_fill, index[u] + 1)
                if kind == "X":
                    t = n * CT + g
                    dve.wait_ge(s_xhi, t + 1)
                    cols = slice(g * P, (g + 1) * P)
                    dve.tensor_tensor(xT[:, n % 2, 1, :, cols], bank.rearrange("p (g r) -> p g r", g=NG),
                                      xT[:, n % 2, 0, :, cols].bitcast(F32), ALU.subtract).then_inc(s_ev, 1)
                    if g < 2:
                        norm2(t + 2)
                elif kind == "Y":
                    t = n * CT + g
                    dve.tensor_tensor(x_sb[:, t, :], bank, x_sb[:, t, :], ALU.add).then_inc(s_ev, 1)
                else:
                    if kind == "D":
                        dst = yT[:, n // NI % 2, g, :]
                        wait_read(dve, ("D", n - 1, g))
                    else:
                        a = "GU".index(kind)
                        dst = acc[:, n % 2, a, 0, :]
                        if g == 2:
                            dve.wait_ge(s_add, 2 * n + a + 1)
                        else:
                            wait_read(dve, (kind, n, g - 1))
                    dve.scalar_tensor_tensor(dst, bank, scale_of(u), dst, ALU.mult, ALU.add).then_inc(s_ev, 1)


_INS = ["x", "ctx_4096", "L0_xattn_Wq", "L0_xattn_bq", "L0_xattn_Wk", "L0_xattn_bk", "L0_xattn_Wv", "L0_xattn_bv",
        "L0_xattn_Wo", "L0_xattn_bo", "L0_ffn_gate_w", "L0_ffn_gate_z", "L0_ffn_gate_s", "L0_ffn_up_w",
        "L0_ffn_up_z", "L0_ffn_up_s", "L0_ffn_down_w", "L0_ffn_down_z", "L0_ffn_down_s"]


def kernel(**inputs):
    import numpy as np
    import concourse.bacc as bacc
    from concourse.bass_utils import run_bass_kernel_spmd

    nc = bacc.Bacc("TRN2", target_bir_lowering=False, num_devices=1)
    arrays, args = {}, []
    for name in _INS:
        a = np.ascontiguousarray(inputs[name])
        arrays[f"in_{name}"] = a
        args.append(nc.dram_tensor(f"in_{name}", a.shape, mybir.dt.from_np(a.dtype), kind="ExternalInput").ap())
    out = nc.dram_tensor("out", arrays["in_x"].shape, F32, kind="ExternalOutput").ap()
    xattn_ffn(nc, *args, out)
    return run_bass_kernel_spmd(nc, [arrays], core_ids=[0]).results[0]["out"]
```

```python
from contextlib import ExitStack

import concourse.bass as bass
from concourse import mybir

F32 = mybir.dt.float32
F32R = mybir.dt.float32r
I32 = mybir.dt.int32
ALU = mybir.AluOpType
ACT = mybir.ActivationFunctionType
AX_X = mybir.AxisListType.X

P = 128
EPS = 1e-5


def xattn_ffn(nc, x, ctx, Wq, bq, Wk, bk, Wv, bv, Wo, bo,
              gate_w, gate_z, gate_s, up_w, up_z, up_s, down_w, down_z, down_s, out):
    B, D, L = x.shape
    Lh = 64
    NC = L // P
    NT = B * D // P
    I = gate_w.shape[1]
    NG = L // P
    NI = I // P
    CT = 4
    NCH = NT // CT
    CR = CT * P
    NS = NCH * NI
    SCALE = 1.0 / Lh ** 0.5
    assert 2 * D == P and L == 512 and CR == 512 and down_w.shape == (I, L)

    HALF = I // 2
    z_gu = nc.dram_tensor("z_gu", [4 * NG, HALF], F32, kind="Internal").ap()
    z_d = nc.dram_tensor("z_d", [NI, L], F32, kind="Internal").ap()
    pieces = []
    for m, w in enumerate((gate_w, up_w)):
        for g in range(NG):
            for a in range(2):
                cols = slice(a * HALF, (a + 1) * HALF)
                k = len(pieces)
                pieces.append((w[g * P:(g + 1) * P, cols], z_gu[k:k + 1, :], HALF, ("gu", m, g, cols)))
    NGU = len(pieces)
    for g in range(NI):
        pieces.append((down_w[g * P:(g + 1) * P, :], z_d[g:g + 1, :], L, ("d", 0, g, slice(0, L))))
    RING = 3
    CTXB = 2
    HELP = [(), (1,)]
    LAG = 3
    ORDER = [("G", 0), ("U", 0), ("G", 1), ("U", 1), ("silu", 0), ("G", 2), ("U", 2), ("D", 0), ("D", 1),
             ("G", 3), ("U", 3), ("D", 2), ("D", 3), ("high", 0)]

    with ExitStack() as keep:
        def sem(name):
            return keep.enter_context(nc.semaphore(name))

        def sb(name, shape, dt=F32, stack=keep):
            return stack.enter_context(nc.sbuf_tensor(name, shape, dt))

        x_sb = sb("x_sb", [P, NT, L])
        wgu = sb("wgu", [P, 2, NG, I], F32R)
        wd = sb("wd", [P, NI, L], F32R)
        xT = sb("xT", [P, 2, 2, NG, CR], F32R)
        xn2 = sb("xn2", [P, 2, L])
        wraw = xn2[0:D, 0, 0:4 * D].rearrange("o (m i) -> o m i", m=4)
        s_raw = xn2[:, 1, 0:2 * P].rearrange("r (a p) -> r a p", a=2)
        ident = sb("ident", [P, P])
        wT = sb("wT", [P, 4, P])
        bqk = sb("bqk", [P, 2, D])
        bvo = sb("bvo", [P, 2])
        sgu = sb("sgu", [P, 2, NG, NI])
        sd = sb("sd", [P, NI, NC])
        NSL = NT + 4
        st6 = sb("st6", [P, 2, 6])
        mv = sb("mv", [P, NSL, 2, 2])
        ve = sb("ve", [P, NSL, 2])
        rs = sb("rs", [P, NSL, 2])
        nm = sb("nm", [P, NSL, 2])
        power = sb("power", [P, 2])
        mx = sb("mx", [P, 2 * NC])
        sm = sb("sm", [P, 2 * NC])
        ri = sb("ri", [P, 2 * NC])

        with ExitStack() as s1:
            ctx_sb = sb("ctx_sb", [P, CTXB, L], F32, s1)
            xn = sb("xn", [P, 2, L], F32, s1)
            qT = sb("qT", [P, NC, P], F32, s1)
            kT = sb("kT", [P, NC, P], F32, s1)
            v_sb = sb("v_sb", [P, 2, 2, L], F32, s1)
            pe_ = sb("pe_", [P, NC, 2, Lh], F32, s1)
            p_sb = sb("p_sb", [P, NC, 2, Lh], F32, s1)
            aT = sb("aT", [P, NC, P], F32, s1)
            wq_in = sb("wq_in", [P, RING, HALF], I32, s1)
            wz_in = sb("wz_in", [P, RING, HALF], F32, s1)
            zf = sb("zf", [32 + NI, HALF], F32, s1)
        with ExitStack() as s2:
            acc = sb("acc", [P, 2, 2, 2, CR], F32, s2)
            hr = sb("hr", [P, LAG, 2, CR], F32R, s2)
            h_sb = sb("h_sb", [P, 2, CR], F32, s2)
            yT = sb("yT", [P, 2, NC, CR], F32, s2)
            yadd = sb("yadd", [P, CR], F32, s2)

        banks = keep.enter_context(nc.psum_tensor("banks", [P, 8, 512], F32))
        BQ, BK, BV, BS, BA, BO = 0, 1, 2, 3, 5, 6

        s_wsm = sem("s_wsm")
        s_bias = sem("s_bias")
        s_sc = sem("s_sc")
        s_z = sem("s_z")
        s_zc = sem("s_zc")
        s_zs = sem("s_zs")
        s_id = sem("s_id")
        s_x = [sem(f"s_xin{i}") for i in range(6)]
        s_ctx = [sem(f"s_ctx{i}") for i in range(CTXB)]
        s_w = [sem(f"s_w{i}") for i in range(RING)]
        s_cv = sem("s_cv")
        s_deq = sem("s_deq")
        s_tr = sem("s_tr")
        s_wT = sem("s_wT")
        s_ln = sem("s_ln")
        s_var = sem("s_var")
        s_rs = sem("s_rs")
        s_nm = sem("s_nm")
        s_xn = sem("s_xn")
        s_q = sem("s_q")
        s_k = sem("s_k")
        s_v = sem("s_v")
        s_qe = sem("s_qe")
        s_ke = sem("s_ke")
        s_ve = sem("s_ve")
        s_s = sem("s_s")
        s_mx = sem("s_mx")
        s_sub = sem("s_sub")
        s_exp = sem("s_exp")
        s_sum = sem("s_sum")
        s_ri = sem("s_ri")
        s_p = sem("s_p")
        s_at = sem("s_at")
        s_ate = sem("s_ate")
        s_o = sem("s_o")
        s_x1 = sem("s_x1")
        s_xn2 = sem("s_xn2")
        s_x0 = sem("s_x0")
        s_x0hi = sem("s_x0hi")
        s_x0lo = sem("s_x0lo")
        s_fill = sem("s_fill")
        s_ea = sem("s_ea")
        s_ev = sem("s_ev")
        s_xhi = sem("s_xhi")
        s_silu = sem("s_silu")
        s_hi = sem("s_hi")
        s_add = sem("s_add")
        s_yadd = sem("s_yadd")
        s_h = sem("s_h")
        s_lo = sem("s_lo")
        s_out = sem("s_out")

        def tiles(a):
            return a.rearrange("b d l -> (b d) l").rearrange("(t p) l -> p t l", p=P)

        xf, cf, of = tiles(x), tiles(ctx), tiles(out)
        xparts = [(0, 1), (1, 2), (2, 4), (4, 8), (8, 12), (12, 16)]
        xpart = {t: i for i, (a, b) in enumerate(xparts) for t in range(a, b)}

        work = []
        for n in range(NS + LAG):
            c, it = divmod(n, NI)
            for kind, g in ORDER:
                step = n - {"D": LAG, "silu": 1, "high": 1}.get(kind, 0)
                if 0 <= step < NS:
                    work.append((kind, step, g))
            if c + 1 < NCH and 6 <= it < 6 + CT:
                work.append(("X", c + 1, it - 6))
            if 0 < c < NCH and 3 <= it < 3 + CT:
                work.append(("Y", c - 1, it - 3))
        work += [("Y", NCH - 1, t) for t in range(CT)]
        uses = [u for u in work if u[0] not in ("silu", "high")]
        index = {u: i for i, u in enumerate(uses)}
        EARLY = (BS, BA)
        X0AT = 6

        def held(s):
            return (0 if s < NT else 1), (2 if s >= 4 else 1)

        def helped(n, g):
            return n % NI > 0 and g in HELP[n % len(HELP)]

        def reader(u):
            kind, n, g = u
            if kind in "GU" and g < 2 or kind == "D" and (n % NI == 0 or helped(n, g)):
                return "scalar"
            return "vector"

        freed, count = {}, {"scalar": 0, "vector": 0}
        for u in uses:
            count[reader(u)] += 1
            freed[u] = count[reader(u)]
        read_sem = {"scalar": s_ea, "vector": s_ev}
        helps = {}
        for n in range(NS):
            for g in range(NC):
                if helped(n, g):
                    helps[n, g] = len(helps) + 1

        def wait_read(eng, u):
            eng.wait_ge(read_sem[reader(u)], freed[u])

        def wait_sum(eng, n, g):
            if (n, g) in helps:
                eng.wait_ge(s_yadd, helps[n, g])
            else:
                wait_read(eng, ("D", n, g))

        def scale_of(u):
            kind, n, g = u
            it = n % NI
            return sd[:, it, g:g + 1] if kind == "D" else sgu[:, "GU".index(kind), g, it:it + 1]

        def blocks(bank):
            return banks[:, bank, :].rearrange("p (c r) -> p c r", c=NC)

        block = keep.enter_context(nc.Block())

        zi = zf[:, :].bitcast(I32)

        def rows_of(v, p):
            return v.rearrange("g (t p) -> (g t) p", p=p)

        @block.sync
        def _(sp):
            def load_x(i):
                a, b = xparts[i]
                sp.dma_start(x_sb[:, a:b, :], xf[:, a:b, :]).then_inc(s_x[i], 16)

            def load_ctx(j):
                if j >= CTXB:
                    sp.wait_ge(s_k, j - CTXB + 1)
                    sp.wait_ge(s_v, 2 * (j - CTXB + 1))
                sp.dma_start(ctx_sb[:, j % CTXB, :], cf[:, j, :]).then_inc(s_ctx[j % CTXB], 16)

            def load_piece(k):
                w, z, n, _ = pieces[k]
                if k >= RING:
                    sp.wait_ge(s_deq, k - RING + 1)
                sp.dma_start(wq_in[:, k % RING, 0:n], w).then_inc(s_w[k % RING], 16)
                if k == 0:
                    sp.wait_ge(s_zs, 32)
                sp.dma_start(wz_in[:, k % RING, 0:n], z.partition_broadcast(P)).then_inc(s_w[k % RING], 16)

            def load(s, dst, src):
                sp.dma_start(dst, src).then_inc(s, 16)

            load_x(0)
            load_ctx(0)
            for m, v in enumerate((bq, bk)):
                load(s_bias, bqk[:, m, :], v.rearrange("(a o) -> a o", a=1).partition_broadcast(P))
            load_x(1)
            for h in range(2):
                for m, v in enumerate((bv, bo)):
                    load(s_bias, bvo[h * D:(h + 1) * D, m:m + 1], v.rearrange("(o a) -> o a", a=1))
            load_ctx(1)
            load_x(2)
            zi = zf[:, :].bitcast(I32)
            load(s_z, zi[0:2 * NG, :], rows_of(gate_z, HALF))
            load(s_z, zi[2 * NG:4 * NG, :], rows_of(up_z, HALF))
            load(s_z, zi[32:32 + NI, 0:L], down_z)
            load_x(3)
            load(s_sc, s_raw[0:NG * NI, 0, :], rows_of(gate_s, P))
            load(s_sc, s_raw[NG * NI:2 * NG * NI, 0, :], rows_of(up_s, P))
            load(s_sc, s_raw[0:NI * NC, 1, :], rows_of(down_s, P))
            k = 0
            for j in range(NT):
                if j in (1, 4):
                    load_x(4 + j // 4)
                while k < min(len(pieces), 2 * j + 3):
                    load_piece(k)
                    k += 1
                if j + CTXB < NT:
                    load_ctx(j + CTXB)
            for t in range(NT):
                wait_read(sp, ("Y", t // CT, t % CT))
                sp.dma_start(of[:, t, :], x_sb[:, t, :]).then_inc(s_out, 16)
            sp.wait_ge(s_out, 16 * NT)

        @block.gpsimd
        def _(pool):
            pool.memset(ident[:, :], 0.0).then_inc(s_id, 1)
            pool.wait_ge(s_id, 1)
            pool.affine_select(out=ident[:, :], in_=ident[:, :], compare_op=ALU.not_equal, fill=1.0,
                               base=0, pattern=[[-1, P]], channel_multiplier=1).then_inc(s_id, 1)
            pool.memset(power[:, :], -0.5).then_inc(s_id, 1)
            pool.wait_ge(s_id, 3)

            def rstd(s):
                pool.wait_ge(s_var, s + 1)
                a, b = held(s)
                pool.tensor_tensor(rs[:, s, a:b], ve[:, s, a:b], power[:, 0:b - a], ALU.pow).then_inc(s_rs, 1)

            def dequantise(k):
                _, _, n, (where, m, g, cols) = pieces[k]
                pool.wait_ge(s_cv, k + 1)
                pool.wait_ge(s_w[k % RING], 32 * (k // RING + 1))
                dst = wgu[:, m, g, cols] if where == "gu" else wd[:, g, cols]
                pool.tensor_tensor(dst, wq_in[:, k % RING, 0:n].bitcast(F32), wz_in[:, k % RING, 0:n],
                                   ALU.subtract).then_inc(s_deq, 1)

            for t in range(3):
                rstd(t)
            for j in range(NT):
                for k in range(2 * j, min(2 * j + 2, len(pieces))):
                    dequantise(k)
                rstd(j + 3)
            rstd(NT + 3)

            def add(n):
                for kind in "GU":
                    wait_read(pool, (kind, n, NG - 1))
                pool.tensor_tensor(acc[:, n % 2, :, 0, :], acc[:, n % 2, :, 0, :], acc[:, n % 2, :, 1, :],
                                   ALU.add).then_inc(s_add, 1)

            def product(n):
                pool.wait_ge(s_silu, n + 1)
                pool.wait_ge(s_add, n + 1)
                pool.tensor_tensor(h_sb[:, n % 2, :], acc[:, n % 2, 0, 0, :], acc[:, n % 2, 1, 0, :],
                                   ALU.mult).then_inc(s_h, 1)

            def rest(n):
                pool.wait_ge(s_hi, n + 1)
                pool.tensor_tensor(hr[:, n % LAG, 1, :], h_sb[:, n % 2, :], hr[:, n % LAG, 0, :].bitcast(F32),
                                   ALU.subtract).then_inc(s_lo, 1)

            def help_sum(n, g):
                wait_read(pool, ("D", n, g))
                wait_sum(pool, n - 1, g)
                y = yT[:, n // NI % 2, g, :]
                pool.tensor_tensor(y, y, yadd[:, :], ALU.add).then_inc(s_yadd, 1)

            for n in range(NS + LAG):
                if 1 <= n <= NS:
                    add(n - 1)
                if 2 <= n < NS + 2:
                    rest(n - 2)
                if 1 <= n <= NS:
                    product(n - 1)
                for g in range(NC):
                    if n >= LAG and helped(n - LAG, g):
                        help_sum(n - LAG, g)

        @block.scalar
        def _(act):
            def load(s, dst, src):
                act.dma_start(dst, src).then_inc(s, 16)

            load(s_wsm, wraw[:, 0, :], Wq)
            load(s_wsm, wraw[:, 1, :], Wk)
            load(s_wsm, wraw[:, 3, :], Wv)
            load(s_wsm, wraw[:, 2, :], Wo)

            def zeros():
                act.wait_ge(s_z, 48)
                act.copy(zf[0:4 * NG, :], zi[0:4 * NG, :]).then_inc(s_zc, 1)
                act.copy(zf[32:32 + NI, 0:L], zi[32:32 + NI, 0:L]).then_inc(s_zc, 1)
                act.wait_ge(s_zc, 2)
                load(s_zs, z_gu, zf[0:4 * NG, :])
                load(s_zs, z_d, zf[32:32 + NI, 0:L])

            def take_v(j, b):
                act.wait_ge(s_v, 2 * j + b + 1)
                if j >= 2:
                    act.wait_ge(s_o, j - 1)
                act.activation(v_sb[:, j % 2, b, :], banks[:, BV, :], ACT.Identity,
                               bias=bvo[:, 0:1]).then_inc(s_ve, 1)

            def convert(k):
                if k < len(pieces):
                    n = pieces[k][2]
                    act.wait_ge(s_w[k % RING], 32 * (k // RING + 1))
                    act.copy(wq_in[:, k % RING, 0:n].bitcast(F32), wq_in[:, k % RING, 0:n]).then_inc(s_cv, 1)

            def take_a(j):
                act.wait_ge(s_at, j + 1)
                act.copy(aT[:, :, :], blocks(BA)).then_inc(s_ate, 1)

            def normalise(dst, j, m, s):
                act.wait_ge(s_nm, s + 1)
                return act.activation(dst, x_sb[:, j, :], ACT.Identity, bias=nm[:, s, m:m + 1], scale=rs[:, s, m:m + 1])

            def norm1(j):
                if j >= 2:
                    act.wait_ge(s_q, j - 1)
                normalise(xn[:, j % 2, :], j, 0, j).then_inc(s_xn, 1)

            def norm2(t):
                if t < 2:
                    act.wait_ge(s_tr, 2)
                elif t < CT + 2:
                    act.wait_ge(s_x0, t - 1)
                else:
                    act.wait_ge(s_fill, index[("X", (t - 2) // CT, (t - 2) % CT)] + 1)
                normalise(xn2[:, t % 2, :], t, 1, t + 4).then_inc(s_xn2, 1)

            norm1(0)
            norm1(1)
            zeros()
            act.wait_ge(s_bias, 96)
            take_v(0, 0)
            take_v(0, 1)
            for j in range(NT):
                act.wait_ge(s_sub, j + 1)
                act.activation(pe_[:, :, :, :], pe_[:, :, :, :], ACT.Exp, scale=SCALE).then_inc(s_exp, 1)
                if X0AT <= j < X0AT + CT:
                    t = j - X0AT
                    act.wait_ge(s_x0, t + 1)
                    act.copy(xT[:, 0, 0, :, t * P:(t + 1) * P], blocks(BA)).then_inc(s_x0hi, 1)
                if j + 1 < NT:
                    take_v(j + 1, 0)
                convert(2 * j)
                if j + 1 < NT:
                    take_v(j + 1, 1)
                    take_a(j)
                if j + 2 < NT:
                    norm1(j + 2)
                if X0AT - 1 <= j < X0AT - 1 + CT:
                    norm2(j - X0AT + 1)
                if j + 1 < NT:
                    convert(2 * j + 1)

            def silu(n):
                act.wait_ge(s_add, n + 1)
                act.activation(acc[:, n % 2, 0, 0, :], acc[:, n % 2, 0, 0, :], ACT.Silu).then_inc(s_silu, 1)

            def high(n):
                act.wait_ge(s_h, n + 1)
                if n >= LAG:
                    act.wait_ge(s_fill, index[("D", n - LAG, NC - 1)] + 1)
                act.copy(hr[:, n % LAG, 0, :], h_sb[:, n % 2, :]).then_inc(s_hi, 1)

            for u in work:
                kind, n, g = u
                if kind in ("silu", "high"):
                    (silu if kind == "silu" else high)(n)
                    continue
                i = index[u]
                if i == EARLY[0]:
                    take_a(NT - 1)
                bank = banks[:, i % 8, :]
                if kind == "X":
                    act.wait_ge(s_fill, i + 1)
                    act.copy(xT[:, n % 2, 0, :, g * P:(g + 1) * P], blocks(i % 8)).then_inc(s_xhi, 1)
                    if g < 2:
                        norm2(n * CT + g + 2)
                if kind == "G" and g == 0:
                    c, it = divmod(n, NI)
                    if c + 1 < NCH and it in (4, 5):
                        norm2((c + 1) * CT + it - 4)
                if reader(u) == "scalar":
                    act.wait_ge(s_fill, i + 1)
                    if kind == "D":
                        if n == 0:
                            act.wait_ge(s_deq, len(pieces))
                        dst = yT[:, n // NI % 2, g, :]
                        if helped(n, g):
                            dst = yadd[:, :]
                            if helps[n, g] > 1:
                                act.wait_ge(s_yadd, helps[n, g] - 1)
                    else:
                        dst = acc[:, n % 2, "GU".index(kind), g, :]
                        if kind == "G" and g == 0 and n >= 2:
                            act.wait_ge(s_h, n - 1)
                    act.activation(dst, bank, ACT.Copy, scale=scale_of(u)).then_inc(s_ea, 1)

        @block.tensor
        def _(pe):
            pe.wait_ge(s_id, 2)
            pe.wait_ge(s_wsm, 64)
            for m in range(4):
                for a in range(2):
                    for b in range(2):
                        if a == b or m == 3:
                            mm = pe.matmul(banks[a * D:(a + 1) * D, BS, m * P + b * D:m * P + (b + 1) * D],
                                           wraw[:, m, :], ident[0:D, 0:D], start=True, stop=True)
            mm.then_inc(s_tr, 1)

            def scales():
                pe.wait_ge(s_sc, 48)
                pe.wait_ge(s_ate, 1)
                ng, nd = 2 * NG * NI, NI * NC
                pe.transpose(banks[:, BA, 0:ng], s_raw[0:ng, 0, :], ident[0:ng, 0:ng])
                pe.transpose(banks[:, BA, ng:ng + nd], s_raw[0:nd, 1, :], ident[0:nd, 0:nd]).then_inc(s_tr, 1)

            def project(j):
                c = j % CTXB
                pe.wait_ge(s_xn, j + 1)
                if j >= 1:
                    pe.wait_ge(s_qe, j)
                for b in range(NC):
                    mm = pe.matmul(banks[:, BQ, b * P:(b + 1) * P], xn[:, j % 2, b * P:(b + 1) * P],
                                   wT[:, 0, :], start=True, stop=True)
                mm.then_inc(s_q, 1)
                pe.wait_ge(s_ctx[c], 16 * (j // CTXB + 1))
                for h in range(2):
                    if 2 * j + h > 0:
                        pe.wait_ge(s_ve, 2 * j + h)
                    r = slice(h * D, (h + 1) * D)
                    pe.matmul(banks[:, BV, :], wT[r, 3, :], ctx_sb[r, c, :],
                              start=True, stop=True).then_inc(s_v, 1)
                    if h == 0:
                        if j >= 1:
                            pe.wait_ge(s_ke, j)
                        for b in range(NC):
                            mm = pe.matmul(banks[:, BK, b * P:(b + 1) * P], ctx_sb[:, c, b * P:(b + 1) * P],
                                           wT[:, 1, :], start=True, stop=True)
                        mm.then_inc(s_k, 1)

            def scores(j):
                pe.wait_ge(s_qe, j + 1)
                pe.wait_ge(s_ke, j + 1)
                if j >= 1:
                    pe.wait_ge(s_sub, j)
                for c in range(NC):
                    for h in range(2):
                        r = slice(h * Lh, (h + 1) * Lh)
                        for b in range(2):
                            o = slice(b * D, (b + 1) * D)
                            mm = pe.matmul(banks[o, BS + h, c * D:(c + 1) * D], qT[r, c, o], kT[r, c, o],
                                           start=True, stop=True)
                mm.then_inc(s_s, 1)

            def mix(j):
                pe.wait_ge(s_p, j + 1)
                if j >= 1:
                    pe.wait_ge(s_ate, j)
                if j == 1:
                    pe.wait_ge(s_wT, 2)
                if X0AT <= j < X0AT + CT:
                    pe.wait_ge(s_x0lo, j - X0AT + 1)
                for c in range(NC):
                    mm = pe.matmul(banks[:, BA, c * P:(c + 1) * P],
                                   p_sb[:, c, :, :].rearrange("p h e -> p (h e)"), wT[:, 2, :],
                                   start=True, stop=True)
                mm.then_inc(s_at, 1)

            def apply(j):
                pe.wait_ge(s_ate, j + 1)
                pe.wait_ge(s_ve, 2 * j + 2)
                if j >= 1:
                    pe.wait_ge(s_x1, j)
                for c in range(NC):
                    for h in range(2):
                        r = slice(h * Lh, (h + 1) * Lh)
                        for b in range(2):
                            o = slice(b * D, (b + 1) * D)
                            lo = (2 * c + h) * Lh
                            mm = pe.matmul(banks[o, BO + h, c * Lh:(c + 1) * Lh], aT[r, c, o],
                                           v_sb[r, j % 2, b, lo:lo + Lh], start=True, stop=True)
                mm.then_inc(s_o, 1)

            def x0(t):
                pe.wait_ge(s_ate, t + X0AT)
                pe.wait_ge(s_xn2, t + 1)
                for g in range(NG):
                    mm = pe.transpose(banks[:, BA, g * P:(g + 1) * P], xn2[:, t % 2, g * P:(g + 1) * P], ident[:, :])
                mm.then_inc(s_x0, 1)

            last = {BQ: (s_qe, NT), BK: (s_ke, NT), BV: (s_ve, 2 * NT), BS: (s_sub, NT), BS + 1: (s_sub, NT),
                    BA: (s_ate, NT), BO: (s_x1, NT), BO + 1: (s_x1, NT)}

            def use(i):
                kind, n, g = uses[i]
                bank = banks[:, i % 8, :]
                if i >= 8:
                    wait_read(pe, uses[i - 8])
                else:
                    pe.wait_ge(*last[i])
                if kind == "X":
                    pe.wait_ge(s_xn2, n * CT + g + 1)
                    for b in range(NG):
                        mm = pe.transpose(bank[:, b * P:(b + 1) * P], xn2[:, g % 2, b * P:(b + 1) * P], ident[:, :])
                elif kind == "Y":
                    if g == 0:
                        for b in range(NC):
                            wait_sum(pe, n * NI + NI - 1, b)
                    for b in range(NC):
                        mm = pe.transpose(bank[:, b * P:(b + 1) * P], yT[:, n % 2, b, g * P:(g + 1) * P], ident[:, :])
                else:
                    c, it = divmod(n, NI)
                    if kind == "D":
                        if g == 0:
                            pe.wait_ge(s_lo, n + 1)
                        if n < NI:
                            pe.wait_ge(s_deq, NGU + it + 1)
                        w = wd[:, it, g * P:(g + 1) * P]
                        parts = [hr[:, n % LAG, part, :] for part in range(2)]
                    else:
                        if kind == "G" and g == 0 and it == 0 and c > 0:
                            wait_read(pe, ("X", c, CT - 1))
                        w = wgu[:, "GU".index(kind), g, it * P:(it + 1) * P]
                        parts = [xT[:, c % 2, part, g, :] for part in range(2)]
                    pe.matmul(bank, w, parts[0], start=True, stop=False)
                    mm = pe.matmul(bank, w, parts[1], start=False, stop=True)
                mm.then_inc(s_fill, 1)

            pe.wait_ge(s_wT, 1)
            project(0)
            for j in range(NT):
                scores(j)
                if j >= 1:
                    apply(j - 1)
                if j == 1:
                    scales()
                if X0AT <= j < X0AT + CT:
                    x0(j - X0AT)
                if j + 1 < NT:
                    project(j + 1)
                    mix(j)
            pe.wait_ge(s_deq, NGU)
            pe.wait_ge(s_x0lo, CT)
            for i in range(EARLY[0]):
                use(i)
            mix(NT - 1)
            for i in range(EARLY[0], EARLY[1]):
                use(i)
            apply(NT - 1)
            for i in range(EARLY[1], len(uses)):
                use(i)

        @block.vector
        def _(dve):
            steps = [0]

            def small_step(ins):
                steps[0] += 1
                ins.then_inc(s_ln, 1)
                return steps[0]

            def stats(m, j):
                if m == 0:
                    dve.wait_ge(s_x[xpart[j]], 16)
                else:
                    dve.wait_ge(s_x1, j + 1)
                return m, small_step(dve.bn_stats(st6[:, m, :], x_sb[:, j, :]))

            def finish(s, found):
                for m, n in found:
                    dve.wait_ge(s_ln, n)
                    n = small_step(dve.bn_aggr(mv[:, s, m, :], st6[:, m, :]))
                dve.wait_ge(s_ln, n)
                a, b = held(s)
                dve.tensor_scalar(ve[:, s, a:b], mv[:, s, a:b, 1], EPS, None, ALU.add).then_inc(s_var, 1)

            def shift(s):
                dve.wait_ge(s_rs, s + 1)
                a, b = held(s)
                dve.scalar_tensor_tensor(nm[:, s, a:b], mv[:, s, a:b, 0], -1.0, rs[:, s, a:b],
                                         ALU.mult, ALU.mult).then_inc(s_nm, 1)

            def take(bank, dst, m, there, done, j):
                dve.wait_ge(there, j + 1)
                dve.tensor_tensor(dst[:, :, :].rearrange("p c (b o) -> p (c b) o", b=2),
                                  banks[:, bank, :].rearrange("p (c o) -> p c o", o=D),
                                  bqk[:, m:m + 1, :].to_broadcast([P, 2 * NC, D]), ALU.add).then_inc(done, 1)

            def heads(t):
                return t[:, :].rearrange("p (h c) -> p h c", h=2)

            def spread(t):
                return heads(t).unsqueeze(3).to_broadcast([P, 2, NC, D])

            S = banks[:, BS:BS + 2, 0:NC * D].rearrange("p h (c e) -> p h c e", e=D)
            E = pe_[:, :, :, :].rearrange("p c h e -> p h c e")
            PR = p_sb[:, :, :, :].rearrange("p c h e -> p h c e")

            def less_max(j):
                dve.wait_ge(s_s, j + 1)
                dve.tensor_reduce(heads(mx), S, AX_X, ALU.max).then_inc(s_mx, 1)
                dve.wait_ge(s_mx, j + 1)
                dve.tensor_tensor(E, S, spread(mx), ALU.subtract).then_inc(s_sub, 1)

            def total(j):
                dve.wait_ge(s_exp, j + 1)
                dve.tensor_reduce(heads(sm), E, AX_X, ALU.add).then_inc(s_sum, 1)

            def invert(j):
                dve.wait_ge(s_sum, j + 1)
                dve.reciprocal(ri[:, :], sm[:, :]).then_inc(s_ri, 1)

            def divide(j):
                dve.wait_ge(s_ri, j + 1)
                if j >= 1:
                    dve.wait_ge(s_at, j)
                dve.tensor_tensor(PR, E, spread(ri), ALU.mult).then_inc(s_p, 1)

            def residual(j):
                dve.wait_ge(s_o, j + 1)
                xv = x_sb[:, j, :].rearrange("p (c h l) -> p h c l", c=NC, h=2)
                for h in range(2):
                    ins = dve.scalar_tensor_tensor(
                        xv[:, h], banks[:, BO + h, 0:NC * Lh].rearrange("p (c l) -> p c l", c=NC),
                        bvo[:, 1:2], xv[:, h], ALU.add, ALU.add)
                ins.then_inc(s_x1, 1)

            cleared = small_step(dve.memset(wT[:, :, :], 0.0))
            finish(0, [stats(0, 0)])
            finish(1, [stats(0, 1)])
            shift(0)
            shift(1)
            dve.wait_ge(s_tr, 1)
            dve.wait_ge(s_ln, cleared)
            small = blocks(BS)
            for h in range(2):
                r = slice(h * D, (h + 1) * D)
                dve.tensor_copy(wT[r, 0:3, r], small[r, 0:3, r])
            dve.tensor_copy(wT[:, 3, :], small[:, 3, :]).then_inc(s_wT, 1)
            finish(2, [stats(0, 2)])
            shift(2)
            dve.wait_ge(s_bias, 96)
            take(BQ, qT, 0, s_q, s_qe, 0)
            take(BK, kT, 1, s_k, s_ke, 0)

            for j in range(NT):
                less_max(j)
                if j >= 1:
                    residual(j - 1)
                total(j)
                if j + 1 < NT:
                    take(BQ, qT, 0, s_q, s_qe, j + 1)
                invert(j)
                if j == 1:
                    dve.wait_ge(s_tr, 2)
                    ng, nd = 2 * NG * NI, NI * NC
                    dve.tensor_copy(sgu[:, :, :, :].rearrange("p a g t -> p (a g t)"), banks[:, BA, 0:ng])
                    dve.tensor_copy(sd[:, :, :].rearrange("p g c -> p (g c)"), banks[:, BA, ng:ng + nd]).then_inc(s_wT, 1)
                if X0AT <= j < X0AT + CT:
                    t = j - X0AT
                    dve.wait_ge(s_x0hi, t + 1)
                    cols = slice(t * P, (t + 1) * P)
                    dve.tensor_tensor(xT[:, 0, 1, :, cols], blocks(BA),
                                      xT[:, 0, 0, :, cols].bitcast(F32), ALU.subtract).then_inc(s_x0lo, 1)
                found = [stats(1, j - 1)] if j >= 1 else []
                divide(j)
                if j + 1 < NT:
                    take(BK, kT, 1, s_k, s_ke, j + 1)
                if j > 0:
                    shift(j + 2)
                if j + 3 < NT:
                    found.append(stats(0, j + 3))
                finish(j + 3, found)
            residual(NT - 1)
            finish(NT + 3, [stats(1, NT - 1)])
            shift(NT + 2)
            shift(NT + 3)

            for i, u in enumerate(uses):
                kind, n, g = u
                bank = banks[:, i % 8, :]
                if reader(u) == "scalar":
                    continue
                dve.wait_ge(s_fill, i + 1)
                if kind == "X":
                    t = n * CT + g
                    dve.wait_ge(s_xhi, t - CT + 1)
                    cols = slice(g * P, (g + 1) * P)
                    dve.tensor_tensor(xT[:, n % 2, 1, :, cols], blocks(i % 8),
                                      xT[:, n % 2, 0, :, cols].bitcast(F32), ALU.subtract).then_inc(s_ev, 1)
                elif kind == "Y":
                    t = n * CT + g
                    dve.tensor_tensor(x_sb[:, t, :], bank, x_sb[:, t, :], ALU.add).then_inc(s_ev, 1)
                else:
                    if kind == "D":
                        dst = yT[:, n // NI % 2, g, :]
                        wait_sum(dve, n - 1, g)
                    else:
                        a = "GU".index(kind)
                        dst = acc[:, n % 2, a, g - 2, :]
                        wait_read(dve, (kind, n, g - 2))
                    dve.scalar_tensor_tensor(dst, bank, scale_of(u), dst, ALU.mult, ALU.add).then_inc(s_ev, 1)


_INS = ["x", "ctx_4096", "L0_xattn_Wq", "L0_xattn_bq", "L0_xattn_Wk", "L0_xattn_bk", "L0_xattn_Wv", "L0_xattn_bv",
        "L0_xattn_Wo", "L0_xattn_bo", "L0_ffn_gate_w", "L0_ffn_gate_z", "L0_ffn_gate_s", "L0_ffn_up_w",
        "L0_ffn_up_z", "L0_ffn_up_s", "L0_ffn_down_w", "L0_ffn_down_z", "L0_ffn_down_s"]


def kernel(**inputs):
    import numpy as np
    import concourse.bacc as bacc
    from concourse.bass_utils import run_bass_kernel_spmd

    nc = bacc.Bacc("TRN2", target_bir_lowering=False, num_devices=1)
    arrays, args = {}, []
    for name in _INS:
        a = np.ascontiguousarray(inputs[name])
        arrays[f"in_{name}"] = a
        args.append(nc.dram_tensor(f"in_{name}", a.shape, mybir.dt.from_np(a.dtype), kind="ExternalInput").ap())
    out = nc.dram_tensor("out", arrays["in_x"].shape, F32, kind="ExternalOutput").ap()
    xattn_ffn(nc, *args, out)
    return run_bass_kernel_spmd(nc, [arrays], core_ids=[0]).results[0]["out"]
```

```python
from contextlib import ExitStack

import concourse.bass as bass
from concourse import mybir

F32 = mybir.dt.float32
F32R = mybir.dt.float32r
I32 = mybir.dt.int32
ALU = mybir.AluOpType
ACT = mybir.ActivationFunctionType
AX_X = mybir.AxisListType.X

P = 128
EPS = 1e-5


def xattn_ffn(nc, x, ctx, Wq, bq, Wk, bk, Wv, bv, Wo, bo,
              gate_w, gate_z, gate_s, up_w, up_z, up_s, down_w, down_z, down_s, out):
    B, D, L = x.shape
    Lh = 64
    NC = L // P
    NT = B * D // P
    I = gate_w.shape[1]
    NG = L // P
    NI = I // P
    CT = 4
    NCH = NT // CT
    CR = CT * P
    NS = NCH * NI
    SCALE = 1.0 / Lh ** 0.5
    assert 2 * (NT - 1) == 4 * NG + NI
    assert 2 * D == P and L == 512 and CT == NC and down_w.shape == (I, L)

    HALF = I // 2
    z_gu = nc.dram_tensor("z_gu", [4 * NG, HALF], F32, kind="Internal").ap()
    z_d = nc.dram_tensor("z_d", [NI, L], F32, kind="Internal").ap()
    pieces = []
    for m, w in enumerate((gate_w, up_w)):
        for g in range(NG):
            for a in range(2):
                cols = slice(a * HALF, (a + 1) * HALF)
                k = len(pieces)
                pieces.append((w[g * P:(g + 1) * P, cols], z_gu[k:k + 1, :], HALF, ("gu", m, g, cols)))
    NGU = len(pieces)
    for g in range(NI):
        pieces.append((down_w[g * P:(g + 1) * P, :], z_d[g:g + 1, :], L, ("d", 0, g, slice(0, L))))
    RING = 3
    CTXB = 2
    HELP = [(), (1,)]
    HELP_LAST = (2,)
    LAG = 3
    CHAINED = 3
    ORDER = [("G", 0), ("U", 0), ("G", 1), ("U", 1), ("silu", 0), ("G", 2), ("U", 2), ("D", 0), ("D", 1),
             ("G", 3), ("U", 3), ("D", 2), ("D", 3), ("high", 0)]

    with ExitStack() as keep:
        def sem(name):
            return keep.enter_context(nc.semaphore(name))

        def sb(name, shape, dt=F32, stack=keep):
            return stack.enter_context(nc.sbuf_tensor(name, shape, dt))

        x_sb = sb("x_sb", [P, NT, L])
        wgu = sb("wgu", [P, 2, NG, I], F32R)
        wd = sb("wd", [P, NI, L], F32R)
        xT = sb("xT", [P, 2, 2, NG, CR], F32R)
        xn2 = sb("xn2", [P, 2, L])
        wraw = xn2[0:D, 0, 0:4 * D].rearrange("o (m i) -> o m i", m=4)
        s_raw = xn2[:, 1, 0:2 * P].rearrange("r (a p) -> r a p", a=2)
        ident = sb("ident", [P, P])
        wT = sb("wT", [P, 4, P])
        bqk = sb("bqk", [P, 2, D])
        bvo = sb("bvo", [P, 2])
        sgu = sb("sgu", [P, 2, NG, NI])
        sd = sb("sd", [P, NI, NC])
        NSL = NT + 4
        st6 = sb("st6", [P, 2, 6])
        mv = sb("mv", [P, NSL, 2, 2])
        ve = sb("ve", [P, NSL, 2])
        rs = sb("rs", [P, NSL, 2])
        nm = sb("nm", [P, NSL, 2])
        power = sb("power", [P, 2])
        mx = sb("mx", [P, 2 * NC])
        sm = sb("sm", [P, 2 * NC])
        ri = sb("ri", [P, 2 * NC])

        with ExitStack() as s1:
            ctx_sb = sb("ctx_sb", [P, CTXB, L], F32, s1)
            xn = sb("xn", [P, 2, L], F32, s1)
            qT = sb("qT", [P, NC, P], F32, s1)
            kT = sb("kT", [P, NC, P], F32, s1)
            v_sb = sb("v_sb", [P, 2, L], F32, s1)
            pe_ = sb("pe_", [P, NC, 2, Lh], F32, s1)
            p_sb = sb("p_sb", [P, NC, 2, Lh], F32, s1)
            aT = sb("aT", [P, 2 * NC, D], F32, s1)
            wq_in = sb("wq_in", [P, RING, HALF], I32, s1)
            wz_in = sb("wz_in", [P, RING, HALF], F32, s1)
            zf = sb("zf", [32 + NI, HALF], F32, s1)
        with ExitStack() as s2:
            acc = sb("acc", [P, 2, 2, 2, CR], F32, s2)
            hr = sb("hr", [P, LAG, 2, CR], F32R, s2)
            h_sb = sb("h_sb", [P, 2, CR], F32, s2)
            yT = sb("yT", [P, 2, NC, CR], F32, s2)
            yadd = sb("yadd", [P, CR], F32, s2)

        banks = keep.enter_context(nc.psum_tensor("banks", [P, 8, 512], F32))
        BQ, BK, BV, BS, BA, BO, BX = 0, 1, 2, 3, 5, 6, 7

        s_wsm = sem("s_wsm")
        s_bqk = sem("s_bqk")
        s_bvo = sem("s_bvo")
        s_sc = sem("s_sc")
        s_z = sem("s_z")
        s_zc = sem("s_zc")
        s_zs = sem("s_zs")
        s_id = sem("s_id")
        s_x = [sem(f"s_xin{i}") for i in range(6)]
        s_ctx = [sem(f"s_ctx{i}") for i in range(CTXB)]
        s_w = [sem(f"s_w{i}") for i in range(RING)]
        s_cv = sem("s_cv")
        s_deq = sem("s_deq")
        s_tr = sem("s_tr")
        s_wT = sem("s_wT")
        s_ln = sem("s_ln")
        s_var = sem("s_var")
        s_rs = sem("s_rs")
        s_nm = sem("s_nm")
        s_xn = sem("s_xn")
        s_q = sem("s_q")
        s_k = sem("s_k")
        s_v = sem("s_v")
        s_qe = sem("s_qe")
        s_ke = sem("s_ke")
        s_ve = sem("s_ve")
        s_s = sem("s_s")
        s_mx = sem("s_mx")
        s_sub = sem("s_sub")
        s_exp = sem("s_exp")
        s_sum = sem("s_sum")
        s_ri = sem("s_ri")
        s_p = sem("s_p")
        s_at = sem("s_at")
        s_ate = sem("s_ate")
        s_o = sem("s_o")
        s_x1 = sem("s_x1")
        s_xn2 = sem("s_xn2")
        s_x0 = sem("s_x0")
        s_x0hi = sem("s_x0hi")
        s_x0lo = sem("s_x0lo")
        s_fill = sem("s_fill")
        s_ea = sem("s_ea")
        s_ev = sem("s_ev")
        s_xhi = sem("s_xhi")
        s_silu = sem("s_silu")
        s_hi = sem("s_hi")
        s_add = sem("s_add")
        s_yadd = sem("s_yadd")
        s_h = sem("s_h")
        s_lo = sem("s_lo")
        s_out = sem("s_out")

        def tiles(a):
            return a.rearrange("b d l -> (b d) l").rearrange("(t p) l -> p t l", p=P)

        xf, cf, of = tiles(x), tiles(ctx), tiles(out)
        xparts = [(0, 1), (1, 2), (2, 4), (4, 8), (8, 12), (12, 16)]
        xpart = {t: i for i, (a, b) in enumerate(xparts) for t in range(a, b)}

        work = []
        for n in range(NS + LAG):
            c, it = divmod(n, NI)
            for kind, g in ORDER:
                step = n - {"D": LAG, "silu": 1, "high": 1}.get(kind, 0)
                if 0 <= step < NS:
                    work.append((kind, step, g))
            if c + 1 < NCH and 6 <= it < 6 + CT:
                work.append(("X", c + 1, it - 6))
            if 0 < c < NCH and 3 <= it < 3 + CT:
                work.append(("Y", c - 1, it - 3))
        work += [("Y", NCH - 1, t) for t in range(CT)]
        uses = [u for u in work if u[0] not in ("silu", "high")]
        index = {u: i for i, u in enumerate(uses)}
        EARLY = (5, 5)
        X0AT = 6

        def held(s):
            return (0 if s < NT else 1), (2 if s >= 4 else 1)

        def helped(n, g):
            return n % NI > 0 and g in (HELP[n % len(HELP)] if n < NS - LAG else HELP_LAST)

        def chained(n):
            return n < CHAINED or n == NS - 1

        def reader(u):
            kind, n, g = u
            if kind in "GU" and g < (1 if chained(n) else 2) or kind == "D" and (n % NI == 0 and g < 2 or helped(n, g)):
                return "scalar"
            return "vector"

        freed, count = {}, {"scalar": 0, "vector": 0}
        for u in uses:
            count[reader(u)] += 1
            freed[u] = count[reader(u)]
        read_sem = {"scalar": s_ea, "vector": s_ev}
        added = {n: sum(not chained(m) for m in range(n + 1)) for n in range(NS)}
        helps = {}
        for n in range(NS):
            for g in range(NC):
                if helped(n, g):
                    helps[n, g] = len(helps) + 1

        def wait_read(eng, u):
            eng.wait_ge(read_sem[reader(u)], freed[u])

        def wait_gu(eng, n, kind):
            if chained(n):
                wait_read(eng, (kind, n, NG - 1))
            else:
                eng.wait_ge(s_add, added[n])

        def wait_sum(eng, n, g):
            if (n, g) in helps:
                eng.wait_ge(s_yadd, helps[n, g])
            else:
                wait_read(eng, ("D", n, g))

        def scale_of(u):
            kind, n, g = u
            it = n % NI
            return sd[:, it, g:g + 1] if kind == "D" else sgu[:, "GU".index(kind), g, it:it + 1]

        def blocks(bank):
            return banks[:, bank, :].rearrange("p (c r) -> p c r", c=NC)

        block = keep.enter_context(nc.Block())

        zi = zf[:, :].bitcast(I32)

        def rows_of(v, p):
            return v.rearrange("g (t p) -> (g t) p", p=p)

        @block.sync
        def _(sp):
            def load_x(i):
                a, b = xparts[i]
                sp.dma_start(x_sb[:, a:b, :], xf[:, a:b, :]).then_inc(s_x[i], 16)

            def load_ctx(j):
                if j >= CTXB:
                    sp.wait_ge(s_k, j - CTXB + 1)
                    sp.wait_ge(s_v, j - CTXB + 1)
                sp.dma_start(ctx_sb[:, j % CTXB, :], cf[:, j, :]).then_inc(s_ctx[j % CTXB], 16)

            def load_piece(k):
                w, z, n, _ = pieces[k]
                if k >= RING:
                    sp.wait_ge(s_deq, k - RING + 1)
                sp.dma_start(wq_in[:, k % RING, 0:n], w).then_inc(s_w[k % RING], 16)
                if k == 0:
                    sp.wait_ge(s_zs, 32)
                sp.dma_start(wz_in[:, k % RING, 0:n], z.partition_broadcast(P)).then_inc(s_w[k % RING], 16)

            def load(s, dst, src):
                sp.dma_start(dst, src).then_inc(s, 16)

            load_x(0)
            load_ctx(0)
            load_x(1)
            load_ctx(1)
            load_x(2)
            zi = zf[:, :].bitcast(I32)
            load(s_z, zi[0:2 * NG, :], rows_of(gate_z, HALF))
            load(s_z, zi[2 * NG:4 * NG, :], rows_of(up_z, HALF))
            load(s_z, zi[32:32 + NI, 0:L], down_z)
            load_x(3)
            load(s_sc, s_raw[0:NG * NI, 0, :], rows_of(gate_s, P))
            load(s_sc, s_raw[NG * NI:2 * NG * NI, 0, :], rows_of(up_s, P))
            load(s_sc, s_raw[0:NI * NC, 1, :], rows_of(down_s, P))
            k = 0
            for j in range(NT):
                if j in (1, 4):
                    load_x(4 + j // 4)
                if j + CTXB < NT:
                    load_ctx(j + CTXB)
                while k < min(len(pieces), 2 * j + 1):
                    load_piece(k)
                    k += 1
            for t in range(NT - CT):
                wait_read(sp, ("Y", t // CT, t % CT))
                sp.dma_start(of[:, t, :], x_sb[:, t, :]).then_inc(s_out, 16)
            for b in range(NC):
                wait_read(sp, ("Y", NCH - 1, b))
                cols = slice(b * P, (b + 1) * P)
                sp.dma_start(of[:, NT - CT:, cols], x_sb[:, NT - CT:, cols]).then_inc(s_out, 16)
            sp.wait_ge(s_out, 16 * NT)

        @block.gpsimd
        def _(pool):
            pool.memset(ident[:, :], 0.0).then_inc(s_id, 1)
            pool.wait_ge(s_id, 1)
            pool.affine_select(out=ident[:, :], in_=ident[:, :], compare_op=ALU.not_equal, fill=1.0,
                               base=0, pattern=[[-1, P]], channel_multiplier=1).then_inc(s_id, 1)
            pool.memset(power[:, :], -0.5).then_inc(s_id, 1)
            for h in range(2):
                for m, v in enumerate((bv, bo)):
                    pool.dma_start(bvo[h * D:(h + 1) * D, m:m + 1], v.rearrange("(o a) -> o a", a=1)).then_inc(s_bvo, 16)
            pool.wait_ge(s_id, 3)

            def rstd(s):
                pool.wait_ge(s_var, s + 1)
                a, b = held(s)
                pool.tensor_tensor(rs[:, s, a:b], ve[:, s, a:b], power[:, 0:b - a], ALU.pow).then_inc(s_rs, 1)

            def dequantise(k):
                _, _, n, (where, m, g, cols) = pieces[k]
                pool.wait_ge(s_cv, k + 1)
                pool.wait_ge(s_w[k % RING], 32 * (k // RING + 1))
                dst = wgu[:, m, g, cols] if where == "gu" else wd[:, g, cols]
                pool.tensor_tensor(dst, wq_in[:, k % RING, 0:n].bitcast(F32), wz_in[:, k % RING, 0:n],
                                   ALU.subtract).then_inc(s_deq, 1)

            for t in range(3):
                rstd(t)
            for j in range(NT):
                if j >= 1:
                    dequantise(2 * j - 2)
                    dequantise(2 * j - 1)
                rstd(j + 3)

            def add(n):
                for kind in "GU":
                    wait_read(pool, (kind, n, NG - 1))
                pool.tensor_tensor(acc[:, n % 2, :, 0, :], acc[:, n % 2, :, 0, :], acc[:, n % 2, :, 1, :],
                                   ALU.add).then_inc(s_add, 1)

            def product(n):
                pool.wait_ge(s_silu, n + 1)
                wait_gu(pool, n, "U")
                pool.tensor_tensor(h_sb[:, n % 2, :], acc[:, n % 2, 0, 0, :], acc[:, n % 2, 1, 0, :],
                                   ALU.mult).then_inc(s_h, 1)

            def rest(n):
                pool.wait_ge(s_hi, n + 1)
                pool.tensor_tensor(hr[:, n % LAG, 1, :], h_sb[:, n % 2, :], hr[:, n % LAG, 0, :].bitcast(F32),
                                   ALU.subtract).then_inc(s_lo, 1)

            def help_sum(n, g):
                wait_read(pool, ("D", n, g))
                wait_sum(pool, n - 1, g)
                y = yT[:, n // NI % 2, g, :]
                pool.tensor_tensor(y, y, yadd[:, :], ALU.add).then_inc(s_yadd, 1)

            for n in range(NS + LAG):
                if 1 <= n <= NS and not chained(n - 1):
                    add(n - 1)
                if n == 2:
                    rstd(NT + 3)
                if 2 <= n < NS + 2:
                    rest(n - 2)
                if 1 <= n <= NS:
                    product(n - 1)
                for g in range(NC):
                    if n >= LAG and helped(n - LAG, g):
                        help_sum(n - LAG, g)

        @block.scalar
        def _(act):
            def load(s, dst, src):
                act.dma_start(dst, src).then_inc(s, 16)

            load(s_wsm, wraw[:, 0, :], Wq)
            load(s_wsm, wraw[:, 1, :], Wk)
            load(s_wsm, wraw[:, 3, :], Wv)
            load(s_wsm, wraw[:, 2, :], Wo)
            for m, v in enumerate((bq, bk)):
                load(s_bqk, bqk[:, m, :], v.rearrange("(a o) -> a o", a=1).partition_broadcast(P))

            def zeros():
                act.wait_ge(s_z, 48)
                act.copy(zf[0:4 * NG, :], zi[0:4 * NG, :]).then_inc(s_zc, 1)
                act.copy(zf[32:32 + NI, 0:L], zi[32:32 + NI, 0:L]).then_inc(s_zc, 1)
                act.wait_ge(s_zc, 2)
                load(s_zs, z_gu, zf[0:4 * NG, :])
                load(s_zs, z_d, zf[32:32 + NI, 0:L])

            def take_v(j):
                act.wait_ge(s_v, j + 1)
                if j >= 2:
                    act.wait_ge(s_o, j - 1)
                act.activation(v_sb[:, j % 2, :], banks[:, BV, :], ACT.Identity, bias=bvo[:, 0:1]).then_inc(s_ve, 1)

            def convert(k):
                n = pieces[k][2]
                act.wait_ge(s_w[k % RING], 32 * (k // RING + 1))
                act.copy(wq_in[:, k % RING, 0:n].bitcast(F32), wq_in[:, k % RING, 0:n]).then_inc(s_cv, 1)

            def take_a(j):
                act.wait_ge(s_at, j + 1)
                act.copy(aT[:, :, :].rearrange("p h o -> p (h o)"), banks[:, BA, :]).then_inc(s_ate, 1)

            def normalise(dst, j, m, s):
                act.wait_ge(s_nm, s + 1)
                return act.activation(dst, x_sb[:, j, :], ACT.Identity, bias=nm[:, s, m:m + 1], scale=rs[:, s, m:m + 1])

            def norm1(j):
                if j >= 2:
                    act.wait_ge(s_q, j - 1)
                normalise(xn[:, j % 2, :], j, 0, j).then_inc(s_xn, 1)

            def norm2(t):
                if t < 2:
                    act.wait_ge(s_tr, 2)
                elif t < CT + 2:
                    act.wait_ge(s_x0, t - 1)
                else:
                    act.wait_ge(s_fill, index[("X", (t - 2) // CT, (t - 2) % CT)] + 1)
                normalise(xn2[:, t % 2, :], t, 1, t + 4).then_inc(s_xn2, 1)

            norm1(0)
            act.wait_ge(s_bvo, 64)
            take_v(0)
            norm1(1)
            zeros()
            for j in range(NT):
                act.wait_ge(s_sub, j + 1)
                act.activation(pe_[:, :, :, :], pe_[:, :, :, :], ACT.Exp, scale=SCALE).then_inc(s_exp, 1)
                if X0AT <= j < X0AT + CT:
                    t = j - X0AT
                    act.wait_ge(s_x0, t + 1)
                    act.copy(xT[:, 0, 0, :, t * P:(t + 1) * P], blocks(BX)).then_inc(s_x0hi, 1)
                if j + 1 < NT:
                    take_v(j + 1)
                if j >= 1:
                    convert(2 * j - 2)
                if j + 1 < NT:
                    take_a(j)
                if j + 2 < NT:
                    norm1(j + 2)
                if X0AT - 1 <= j < X0AT - 1 + CT:
                    norm2(j - X0AT + 1)
                if j >= 1:
                    convert(2 * j - 1)

            def silu(n):
                wait_gu(act, n, "G")
                act.activation(acc[:, n % 2, 0, 0, :], acc[:, n % 2, 0, 0, :], ACT.Silu).then_inc(s_silu, 1)

            def high(n):
                act.wait_ge(s_h, n + 1)
                if n >= LAG:
                    act.wait_ge(s_fill, index[("D", n - LAG, NC - 1)] + 1)
                act.copy(hr[:, n % LAG, 0, :], h_sb[:, n % 2, :]).then_inc(s_hi, 1)

            for u in work:
                kind, n, g = u
                if kind in ("silu", "high"):
                    (silu if kind == "silu" else high)(n)
                    continue
                i = index[u]
                if i == EARLY[0]:
                    take_a(NT - 1)
                bank = banks[:, i % 8, :]
                if kind == "X":
                    act.wait_ge(s_fill, i + 1)
                    act.copy(xT[:, n % 2, 0, :, g * P:(g + 1) * P], blocks(i % 8)).then_inc(s_xhi, 1)
                    if g < 2:
                        norm2(n * CT + g + 2)
                if kind == "G" and g == 0:
                    c, it = divmod(n, NI)
                    if c + 1 < NCH and it in (4, 5):
                        norm2((c + 1) * CT + it - 4)
                if reader(u) == "scalar":
                    act.wait_ge(s_fill, i + 1)
                    if kind == "D":
                        if n == 0:
                            act.wait_ge(s_deq, len(pieces))
                        dst = yT[:, n // NI % 2, g, :]
                        if helped(n, g):
                            dst = yadd[:, :]
                            if helps[n, g] > 1:
                                act.wait_ge(s_yadd, helps[n, g] - 1)
                    else:
                        dst = acc[:, n % 2, "GU".index(kind), g, :]
                        if kind == "G" and g == 0 and n >= 2:
                            act.wait_ge(s_h, n - 1)
                    act.activation(dst, bank, ACT.Copy, scale=scale_of(u)).then_inc(s_ea, 1)

        @block.tensor
        def _(pe):
            pe.wait_ge(s_id, 2)
            pe.wait_ge(s_wsm, 64)
            for m in range(4):
                for h in range(2):
                    r = slice(h * D, (h + 1) * D)
                    mm = pe.matmul(banks[r, BS, m * P + h * D:m * P + (h + 1) * D], wraw[:, m, :], ident[0:D, 0:D],
                                   start=True, stop=True)
            mm.then_inc(s_tr, 1)

            HALVES = [slice(b * D, (b + 1) * D) for b in range(2)]
            TURNS = [(0, 0), (0, 1), (1, 0), (1, 1)]

            def scales():
                pe.wait_ge(s_sc, 48)
                ng, nd = 2 * NG * NI, NI * NC
                pe.transpose(banks[:, BX, 0:ng], s_raw[0:ng, 0, :], ident[0:ng, 0:ng])
                pe.transpose(banks[:, BX, ng:ng + nd], s_raw[0:nd, 1, :], ident[0:nd, 0:nd]).then_inc(s_tr, 1)

            def project(j):
                pe.wait_ge(s_xn, j + 1)
                if j >= 1:
                    pe.wait_ge(s_qe, j)
                for b in range(NC):
                    mm = pe.matmul(banks[:, BQ, b * P:(b + 1) * P], xn[:, j % 2, b * P:(b + 1) * P],
                                   wT[:, 0, :], start=True, stop=True)
                mm.then_inc(s_q, 1)
                c = j % CTXB
                pe.wait_ge(s_ctx[c], 16 * (j // CTXB + 1))
                if j >= 1:
                    pe.wait_ge(s_ve, j)
                pe.matmul(banks[:, BV, :], wT[:, 3, :], ctx_sb[:, c, :], start=True, stop=True).then_inc(s_v, 1)
                if j >= 1:
                    pe.wait_ge(s_ke, j)
                for b in range(NC):
                    mm = pe.matmul(banks[:, BK, b * P:(b + 1) * P], ctx_sb[:, c, b * P:(b + 1) * P],
                                   wT[:, 1, :], start=True, stop=True)
                mm.then_inc(s_k, 1)

            def scores(j):
                pe.wait_ge(s_qe, j + 1)
                pe.wait_ge(s_ke, j + 1)
                if j >= 1:
                    pe.wait_ge(s_sub, j)
                for c in range(NC):
                    for b, h in TURNS:
                        r = slice(h * Lh, (h + 1) * Lh)
                        o = slice(b * D, (b + 1) * D)
                        mm = pe.matmul(banks[o, BS + h, c * D:(c + 1) * D], qT[r, c, o], kT[r, c, o],
                                       start=True, stop=True)
                mm.then_inc(s_s, 1)

            def mix(j):
                pe.wait_ge(s_p, j + 1)
                if j >= 1:
                    pe.wait_ge(s_ate, j)
                for c in range(NC):
                    for h in range(2):
                        for r in HALVES:
                            mm = pe.matmul(banks[r, BA, (2 * c + h) * D:(2 * c + h + 1) * D], p_sb[r, c, h, :],
                                           wT[r, 2, r], start=True, stop=True)
                mm.then_inc(s_at, 1)

            def apply(j):
                pe.wait_ge(s_ate, j + 1)
                pe.wait_ge(s_ve, j + 1)
                if j >= 1:
                    pe.wait_ge(s_x1, j)
                for h in range(2 * NC):
                    for r in HALVES:
                        mm = pe.matmul(banks[r, BO, h * Lh:(h + 1) * Lh], aT[r, h, :],
                                       v_sb[r, j % 2, h * Lh:(h + 1) * Lh], start=True, stop=True)
                mm.then_inc(s_o, 1)

            def x0(t):
                if t > 0:
                    pe.wait_ge(s_x0lo, t)
                else:
                    pe.wait_ge(s_wT, 2)
                pe.wait_ge(s_xn2, t + 1)
                for g in range(NG):
                    mm = pe.transpose(banks[:, BX, g * P:(g + 1) * P], xn2[:, t % 2, g * P:(g + 1) * P], ident[:, :])
                mm.then_inc(s_x0, 1)

            last = {BQ: (s_qe, NT), BK: (s_ke, NT), BV: (s_ve, NT), BS: (s_sub, NT), BS + 1: (s_sub, NT),
                    BA: (s_ate, NT), BO: (s_x1, NT), BX: (s_x0lo, CT)}

            def use(i):
                kind, n, g = uses[i]
                bank = banks[:, i % 8, :]
                if i >= 8:
                    wait_read(pe, uses[i - 8])
                else:
                    pe.wait_ge(*last[i])
                if kind == "X":
                    pe.wait_ge(s_xn2, n * CT + g + 1)
                    for b in range(NG):
                        mm = pe.transpose(bank[:, b * P:(b + 1) * P], xn2[:, g % 2, b * P:(b + 1) * P], ident[:, :])
                elif kind == "Y" and n < NCH - 1:
                    if g == 0:
                        for b in range(NC):
                            wait_sum(pe, n * NI + NI - 1, b)
                    for b in range(NC):
                        mm = pe.transpose(bank[:, b * P:(b + 1) * P], yT[:, n % 2, b, g * P:(g + 1) * P], ident[:, :])
                elif kind == "Y":
                    wait_sum(pe, n * NI + NI - 1, g)
                    for t in range(CT):
                        mm = pe.transpose(bank[:, t * P:(t + 1) * P], yT[:, n % 2, g, t * P:(t + 1) * P], ident[:, :])
                else:
                    c, it = divmod(n, NI)
                    if kind == "D":
                        if g == 0:
                            pe.wait_ge(s_lo, n + 1)
                        if n < NI:
                            pe.wait_ge(s_deq, NGU + it + 1)
                        w = wd[:, it, g * P:(g + 1) * P]
                        parts = [hr[:, n % LAG, part, :] for part in range(2)]
                    else:
                        if kind == "G" and g == 0 and it == 0 and c > 0:
                            wait_read(pe, ("X", c, CT - 1))
                        w = wgu[:, "GU".index(kind), g, it * P:(it + 1) * P]
                        parts = [xT[:, c % 2, part, g, :] for part in range(2)]
                    pe.matmul(bank, w, parts[0], start=True, stop=False)
                    mm = pe.matmul(bank, w, parts[1], start=False, stop=True)
                mm.then_inc(s_fill, 1)

            pe.wait_ge(s_wT, 1)
            project(0)
            for j in range(NT):
                scores(j)
                if j >= 1:
                    apply(j - 1)
                if j == 1:
                    scales()
                if X0AT <= j < X0AT + CT:
                    x0(j - X0AT)
                if j + 1 < NT:
                    project(j + 1)
                    mix(j)
            pe.wait_ge(s_deq, NGU)
            pe.wait_ge(s_x0lo, CT)
            for i in range(EARLY[0]):
                use(i)
            mix(NT - 1)
            for i in range(EARLY[0], EARLY[1]):
                use(i)
            apply(NT - 1)
            for i in range(EARLY[1], len(uses)):
                use(i)

        @block.vector
        def _(dve):
            steps = [0]

            def small_step(ins):
                steps[0] += 1
                ins.then_inc(s_ln, 1)
                return steps[0]

            def stats(m, j):
                if m == 0:
                    dve.wait_ge(s_x[xpart[j]], 16)
                else:
                    dve.wait_ge(s_x1, j + 1)
                return m, small_step(dve.bn_stats(st6[:, m, :], x_sb[:, j, :]))

            def finish(s, found):
                for m, n in found:
                    dve.wait_ge(s_ln, n)
                    n = small_step(dve.bn_aggr(mv[:, s, m, :], st6[:, m, :]))
                dve.wait_ge(s_ln, n)
                a, b = held(s)
                dve.tensor_scalar(ve[:, s, a:b], mv[:, s, a:b, 1], EPS, None, ALU.add).then_inc(s_var, 1)

            def shift(s):
                dve.wait_ge(s_rs, s + 1)
                a, b = held(s)
                dve.scalar_tensor_tensor(nm[:, s, a:b], mv[:, s, a:b, 0], -1.0, rs[:, s, a:b],
                                         ALU.mult, ALU.mult).then_inc(s_nm, 1)

            def take(bank, dst, m, there, done, j):
                dve.wait_ge(there, j + 1)
                dve.tensor_tensor(dst[:, :, :].rearrange("p c (b o) -> p (c b) o", b=2),
                                  banks[:, bank, :].rearrange("p (c o) -> p c o", o=D),
                                  bqk[:, m:m + 1, :].to_broadcast([P, 2 * NC, D]), ALU.add).then_inc(done, 1)

            def heads(t):
                return t[:, :].rearrange("p (h c) -> p h c", h=2)

            def spread(t):
                return heads(t).unsqueeze(3).to_broadcast([P, 2, NC, D])

            S = banks[:, BS:BS + 2, 0:NC * D].rearrange("p h (c e) -> p h c e", e=D)
            E = pe_[:, :, :, :].rearrange("p c h e -> p h c e")
            PR = p_sb[:, :, :, :].rearrange("p c h e -> p h c e")

            def less_max(j):
                dve.wait_ge(s_s, j + 1)
                dve.tensor_reduce(heads(mx), S, AX_X, ALU.max).then_inc(s_mx, 1)
                dve.wait_ge(s_mx, j + 1)
                dve.tensor_tensor(E, S, spread(mx), ALU.subtract).then_inc(s_sub, 1)

            def total(j):
                dve.wait_ge(s_exp, j + 1)
                dve.tensor_reduce(heads(sm), E, AX_X, ALU.add).then_inc(s_sum, 1)

            def invert(j):
                dve.wait_ge(s_sum, j + 1)
                dve.reciprocal(ri[:, :], sm[:, :]).then_inc(s_ri, 1)

            def divide(j):
                dve.wait_ge(s_ri, j + 1)
                if j >= 1:
                    dve.wait_ge(s_at, j)
                dve.tensor_tensor(PR, E, spread(ri), ALU.mult).then_inc(s_p, 1)

            def residual(j):
                dve.wait_ge(s_o, j + 1)
                dve.scalar_tensor_tensor(x_sb[:, j, :], banks[:, BO, :], bvo[:, 1:2], x_sb[:, j, :],
                                         ALU.add, ALU.add).then_inc(s_x1, 1)

            cleared = small_step(dve.memset(wT[:, :, :], 0.0))
            finish(0, [stats(0, 0)])
            shift(0)
            dve.wait_ge(s_tr, 1)
            dve.wait_ge(s_ln, cleared)
            small = blocks(BS)
            for h in range(2):
                r = slice(h * D, (h + 1) * D)
                ins = dve.tensor_copy(wT[r, :, r], small[r, :, r])
            ins.then_inc(s_wT, 1)
            finish(1, [stats(0, 1)])
            shift(1)
            finish(2, [stats(0, 2)])
            shift(2)
            dve.wait_ge(s_bqk, 32)
            dve.wait_ge(s_bvo, 64)
            take(BQ, qT, 0, s_q, s_qe, 0)
            take(BK, kT, 1, s_k, s_ke, 0)

            for j in range(NT):
                less_max(j)
                if j >= 1:
                    residual(j - 1)
                total(j)
                invert(j)
                divide(j)
                if j + 1 < NT:
                    take(BQ, qT, 0, s_q, s_qe, j + 1)
                    take(BK, kT, 1, s_k, s_ke, j + 1)
                if j == 1:
                    dve.wait_ge(s_tr, 2)
                    ng, nd = 2 * NG * NI, NI * NC
                    dve.tensor_copy(sgu[:, :, :, :].rearrange("p a g t -> p (a g t)"), banks[:, BX, 0:ng])
                    dve.tensor_copy(sd[:, :, :].rearrange("p g c -> p (g c)"), banks[:, BX, ng:ng + nd]).then_inc(s_wT, 1)
                if X0AT <= j < X0AT + CT:
                    t = j - X0AT
                    dve.wait_ge(s_x0hi, t + 1)
                    cols = slice(t * P, (t + 1) * P)
                    dve.tensor_tensor(xT[:, 0, 1, :, cols], blocks(BX),
                                      xT[:, 0, 0, :, cols].bitcast(F32), ALU.subtract).then_inc(s_x0lo, 1)
                if j >= 1:
                    shift(j + 2)
                found = [stats(1, j - 1)] if j >= 1 else []
                if j + 3 < NT:
                    found.append(stats(0, j + 3))
                finish(j + 3, found)
            residual(NT - 1)
            shift(NT + 2)

            for i, u in enumerate(uses):
                kind, n, g = u
                bank = banks[:, i % 8, :]
                if u == ("G", 1, 2):
                    finish(NT + 3, [stats(1, NT - 1)])
                if u == ("G", 2, 2):
                    shift(NT + 3)
                if reader(u) == "scalar":
                    continue
                dve.wait_ge(s_fill, i + 1)
                if kind == "X":
                    t = n * CT + g
                    dve.wait_ge(s_xhi, t - CT + 1)
                    cols = slice(g * P, (g + 1) * P)
                    dve.tensor_tensor(xT[:, n % 2, 1, :, cols], blocks(i % 8),
                                      xT[:, n % 2, 0, :, cols].bitcast(F32), ALU.subtract).then_inc(s_ev, 1)
                elif kind == "Y" and n == NCH - 1:
                    y = x_sb[:, n * CT:, g * P:(g + 1) * P]
                    dve.tensor_tensor(y, blocks(i % 8), y, ALU.add).then_inc(s_ev, 1)
                elif kind == "Y":
                    t = n * CT + g
                    dve.tensor_tensor(x_sb[:, t, :], bank, x_sb[:, t, :], ALU.add).then_inc(s_ev, 1)
                else:
                    if kind == "D":
                        dst = yT[:, n // NI % 2, g, :]
                        if n == 0:
                            dve.wait_ge(s_deq, len(pieces))
                        if n % NI == 0:
                            dve.tensor_scalar(dst, bank, scale_of(u), None, ALU.mult).then_inc(s_ev, 1)
                            continue
                        wait_sum(dve, n - 1, g)
                    else:
                        a = "GU".index(kind)
                        chains = 1 if chained(n) else 2
                        dst = acc[:, n % 2, a, g % chains, :]
                        wait_read(dve, (kind, n, g - chains))
                    dve.scalar_tensor_tensor(dst, bank, scale_of(u), dst, ALU.mult, ALU.add).then_inc(s_ev, 1)


_INS = ["x", "ctx_4096", "L0_xattn_Wq", "L0_xattn_bq", "L0_xattn_Wk", "L0_xattn_bk", "L0_xattn_Wv", "L0_xattn_bv",
        "L0_xattn_Wo", "L0_xattn_bo", "L0_ffn_gate_w", "L0_ffn_gate_z", "L0_ffn_gate_s", "L0_ffn_up_w",
        "L0_ffn_up_z", "L0_ffn_up_s", "L0_ffn_down_w", "L0_ffn_down_z", "L0_ffn_down_s"]


def kernel(**inputs):
    import numpy as np
    import concourse.bacc as bacc
    from concourse.bass_utils import run_bass_kernel_spmd

    nc = bacc.Bacc("TRN2", target_bir_lowering=False, num_devices=1)
    arrays, args = {}, []
    for name in _INS:
        a = np.ascontiguousarray(inputs[name])
        arrays[f"in_{name}"] = a
        args.append(nc.dram_tensor(f"in_{name}", a.shape, mybir.dt.from_np(a.dtype), kind="ExternalInput").ap())
    out = nc.dram_tensor("out", arrays["in_x"].shape, F32, kind="ExternalOutput").ap()
    xattn_ffn(nc, *args, out)
    return run_bass_kernel_spmd(nc, [arrays], core_ids=[0]).results[0]["out"]
```
